# Optimizing a Trainium2 kernel written in Bass

```python
import numpy as np
import jax
import jax.numpy as jnp

def _softmax(x, axis=-1):
    return jax.nn.softmax(x, axis=axis)

def _gelu(x):
    return jax.nn.gelu(x, approximate=True)

def _silu(x):
    return jax.nn.silu(x)

def _sigmoid(x):
    return jax.nn.sigmoid(x)

def _layernorm(x, axis=-1, eps=1e-05):
    m = jnp.mean(x, axis=axis, keepdims=True)
    v = jnp.var(x, axis=axis, keepdims=True)
    return (x - m) / jnp.sqrt(v + eps)

def _scatter_add(tgt, idx, src, axis=0):
    return tgt.at[idx].add(src)

def _segment_sum(src, seg, n):
    return jax.ops.segment_sum(src, seg, n)
kernel_name = 'mk_seq_postln_d1_jaxref_r8_f66fdf'

def setup_inputs(seed: int=0):
    np.random.seed(seed)
    _w = jnp.asarray

    def _L0_attn_setup():
        import jax, jax.numpy as jnp
        import numpy as np
        import math
        B, T, D = (2, 512, 128)
        H = 16
        HEAD_DIM = D // H
        CHUNK = 64

        def chunked_attention(q, k, v, chunk_size, scale):
            Bq, Hq, Tq, hd = q.shape
            S = k.shape[2]
            nc = Tq // chunk_size
            q_chunks = q.reshape(Bq, Hq, nc, chunk_size, hd).transpose(2, 0, 1, 3, 4)
            starts = jnp.arange(nc, dtype=jnp.int32) * chunk_size
            k_pos = jnp.arange(S)

            def body(carry, xs):
                qc, start = xs
                scores = jnp.einsum('bhqd,bhkd->bhqk', qc, k) * scale
                q_pos = start + jnp.arange(chunk_size)
                causal_mask = k_pos[None, :] > q_pos[:, None]
                scores = jnp.where(causal_mask[None, None], -jnp.inf, scores)
                m = jnp.max(scores, axis=-1, keepdims=True)
                m = jnp.where(jnp.isinf(m), jnp.zeros_like(m), m)
                p = jax.nn.softmax(scores - m, axis=-1)
                oc = jnp.einsum('bhqk,bhkd->bhqd', p, v)
                return (carry, oc)
            _, outs = jax.lax.scan(body, None, (q_chunks, starts))
            return outs.transpose(1, 2, 0, 3, 4).reshape(Bq, Hq, Tq, hd)
        key = jax.random.key(seed)
        ks = jax.random.split(key, 9)
        s = 1.0 / math.sqrt(D)
        return {'x': jax.random.normal(ks[0], (B, T, D), dtype=jnp.float32), 'Wq': jax.random.normal(ks[1], (D, D), dtype=jnp.float32) * s, 'bq': jax.random.normal(ks[2], (D,), dtype=jnp.float32) * 0.01, 'Wk': jax.random.normal(ks[3], (D, D), dtype=jnp.float32) * s, 'bk': jax.random.normal(ks[4], (D,), dtype=jnp.float32) * 0.01, 'Wv': jax.random.normal(ks[5], (D, D), dtype=jnp.float32) * s, 'bv': jax.random.normal(ks[6], (D,), dtype=jnp.float32) * 0.01, 'Wo': jax.random.normal(ks[7], (D, D), dtype=jnp.float32) * s, 'bo': jax.random.normal(ks[8], (D,), dtype=jnp.float32) * 0.01}
    _L0_attn_in = _L0_attn_setup()

    def _L0_ffn_setup():
        import jax, jax.numpy as jnp
        import numpy as np
        S, B, D, FF, E = (128, 2, 128, 256, 8)
        key = jax.random.key(seed)
        ks = jax.random.split(key, 8)
        s = 0.02
        return {'hidden_states': jax.random.normal(ks[0], (S, B, D), dtype=jnp.float32), 'router_w': jax.random.normal(ks[1], (E, D), dtype=jnp.float32) * s, 'expert_gate': jax.random.normal(ks[2], (E, D, FF), dtype=jnp.float32) * s, 'expert_up': jax.random.normal(ks[3], (E, D, FF), dtype=jnp.float32) * s, 'expert_down': jax.random.normal(ks[4], (E, FF, D), dtype=jnp.float32) * s, 'shared_gate': jax.random.normal(ks[5], (D, FF), dtype=jnp.float32) * s, 'shared_up': jax.random.normal(ks[6], (D, FF), dtype=jnp.float32) * s, 'shared_down': jax.random.normal(ks[7], (FF, D), dtype=jnp.float32) * s}
    _L0_ffn_in = _L0_ffn_setup()
    _d = {'L0_attn_x': _L0_attn_in['x'], 'L0_attn_Wq': _L0_attn_in['Wq'], 'L0_attn_bq': _L0_attn_in['bq'], 'L0_attn_Wk': _L0_attn_in['Wk'], 'L0_attn_bk': _L0_attn_in['bk'], 'L0_attn_Wv': _L0_attn_in['Wv'], 'L0_attn_bv': _L0_attn_in['bv'], 'L0_attn_Wo': _L0_attn_in['Wo'], 'L0_attn_bo': _L0_attn_in['bo'], 'L0_ffn_router_w': _L0_ffn_in['router_w'], 'L0_ffn_expert_gate': _L0_ffn_in['expert_gate'], 'L0_ffn_expert_up': _L0_ffn_in['expert_up'], 'L0_ffn_expert_down': _L0_ffn_in['expert_down'], 'L0_ffn_shared_gate': _L0_ffn_in['shared_gate'], 'L0_ffn_shared_up': _L0_ffn_in['shared_up'], 'L0_ffn_shared_down': _L0_ffn_in['shared_down']}
    _x0 = _d['L0_attn_x']
    _d['L0_attn_x'] = jax.random.normal(jax.random.fold_in(jax.random.key(seed), 1), (1, 2048, 128), dtype=_x0.dtype)
    del _x0
    return _d

def reference(L0_attn_x, L0_attn_Wq, L0_attn_bq, L0_attn_Wk, L0_attn_bk, L0_attn_Wv, L0_attn_bv, L0_attn_Wo, L0_attn_bo, L0_ffn_router_w, L0_ffn_expert_gate, L0_ffn_expert_up, L0_ffn_expert_down, L0_ffn_shared_gate, L0_ffn_shared_up, L0_ffn_shared_down):

    def _L0_attn_ref(x, Wq, bq, Wk, bk, Wv, bv, Wo, bo):
        import jax, jax.numpy as jnp
        import numpy as np
        import math
        B, T, D = (2, 512, 128)
        H = 16
        HEAD_DIM = D // H
        CHUNK = 64

        def chunked_attention(q, k, v, chunk_size, scale):
            Bq, Hq, Tq, hd = q.shape
            S = k.shape[2]
            nc = Tq // chunk_size
            q_chunks = q.reshape(Bq, Hq, nc, chunk_size, hd).transpose(2, 0, 1, 3, 4)
            starts = jnp.arange(nc, dtype=jnp.int32) * chunk_size
            k_pos = jnp.arange(S)

            def body(carry, xs):
                qc, start = xs
                scores = jnp.einsum('bhqd,bhkd->bhqk', qc, k) * scale
                q_pos = start + jnp.arange(chunk_size)
                causal_mask = k_pos[None, :] > q_pos[:, None]
                scores = jnp.where(causal_mask[None, None], -jnp.inf, scores)
                m = jnp.max(scores, axis=-1, keepdims=True)
                m = jnp.where(jnp.isinf(m), jnp.zeros_like(m), m)
                p = jax.nn.softmax(scores - m, axis=-1)
                oc = jnp.einsum('bhqk,bhkd->bhqd', p, v)
                return (carry, oc)
            _, outs = jax.lax.scan(body, None, (q_chunks, starts))
            return outs.transpose(1, 2, 0, 3, 4).reshape(Bq, Hq, Tq, hd)
        Bx, Tx, Dx = x.shape
        scale = 1.0 / math.sqrt(HEAD_DIM)

        def proj(W, b):
            y = x @ W.T + b
            return y.reshape(Bx, Tx, H, HEAD_DIM).transpose(0, 2, 1, 3)
        q = proj(Wq, bq)
        k = proj(Wk, bk)
        v = proj(Wv, bv)
        out = chunked_attention(q, k, v, CHUNK, scale)
        out = out.transpose(0, 2, 1, 3).reshape(Bx, Tx, Dx)
        return out @ Wo.T + bo

    def _L0_ffn_ref(hidden_states, router_w, expert_gate, expert_up, expert_down, shared_gate, shared_up, shared_down):
        import jax, jax.numpy as jnp
        import numpy as np
        S, B, D, FF, E = (128, 2, 128, 256, 8)
        seq, bs, d = hidden_states.shape
        n_experts = expert_gate.shape[0]
        x = hidden_states.reshape(-1, d)
        logits = jnp.einsum('td,ed->te', x, router_w)
        top_logit = jnp.max(logits, axis=-1)
        top_idx = jnp.argmax(logits, axis=-1)
        score = jax.nn.sigmoid(top_logit)
        onehot = jax.nn.one_hot(top_idx, n_experts, dtype=x.dtype)
        xs = x * score[:, None]
        g = jnp.einsum('td,edf->etf', xs, expert_gate)
        u = jnp.einsum('td,edf->etf', xs, expert_up)
        h = jax.nn.silu(g) * u
        eo = jnp.einsum('etf,efd->etd', h, expert_down)
        moe_out = jnp.einsum('te,etd->td', onehot, eo)
        sh = jax.nn.silu(x @ shared_gate) * (x @ shared_up) @ shared_down
        return (moe_out + sh).reshape(seq, bs, d)
    x = L0_attn_x
    x = _layernorm(x + _L0_attn_ref(x, L0_attn_Wq, L0_attn_bq, L0_attn_Wk, L0_attn_bk, L0_attn_Wv, L0_attn_bv, L0_attn_Wo, L0_attn_bo), axis=-1)
    x = _layernorm(x + _L0_ffn_ref(x, L0_ffn_router_w, L0_ffn_expert_gate, L0_ffn_expert_up, L0_ffn_expert_down, L0_ffn_shared_gate, L0_ffn_shared_up, L0_ffn_shared_down), axis=-1)
    return x

_drawn_inputs = setup_inputs


def setup_inputs(seed=0):
    import zlib

    import numpy as np

    out = dict(_drawn_inputs(seed))
    spreads = {}
    factors = {'L0_attn_bq': 8.0,
     'L0_attn_bk': 8.0,
     'L0_attn_bv': 5.218,
     'L0_attn_bo': 5.403,
     'L0_ffn_router_w': 8.0,
     'L0_ffn_expert_gate': 8.0,
     'L0_ffn_expert_up': 8.0,
     'L0_ffn_expert_down': 8.0,
     'L0_ffn_shared_gate': 6.941,
     'L0_ffn_shared_up': 6.845,
     'L0_ffn_shared_down': 6.852}
    for name, (base, spread) in spreads.items():
        noise = np.random.default_rng([zlib.crc32(name.encode()), seed]).standard_normal(out[name].shape)
        drawn = base * np.exp(spread * noise) if base else spread * noise
        out[name] = jnp.asarray(drawn.astype(out[name].dtype))
    for name, factor in factors.items():
        out[name] = (out[name] * factor).astype(out[name].dtype)
    return out
```

```python
import struct
from contextlib import ExitStack

import concourse.bass as bass
from concourse import mybir

F32 = mybir.dt.float32
BF16 = mybir.dt.bfloat16
ALU = mybir.AluOpType
ACT = mybir.ActivationFunctionType
AX = mybir.AxisListType

P = 128
BLK = 512
TPB = BLK // P
MASKED = -1.0e30
ONES_PAIR = struct.unpack('<f', bytes.fromhex('803f803f'))[0]
LN_EPS = 1e-5
PARTS = 3
LEAD = 8
RING = 8


def make_plan(NB, G):
    jobs = [(B, g, t, c, hp) for B in range(NB) for g in range(G) for t in range(TPB)
            for c in range(B + 1) for hp in range(2)]
    per_step = [2 * TPB * (B + 1) for B in range(NB) for g in range(G)]
    step_end, at = {}, 0
    for s, n in enumerate(per_step):
        at += n
        step_end[at] = s
    plan, job, pending = [], 0, []

    def score_jobs(upto):
        nonlocal job
        while job < min(upto, len(jobs)):
            plan.append(("scores", job, *jobs[job]))
            job += 1
            for due, s in list(pending):
                if job >= due or job == len(jobs):
                    plan.append(("maxrows", s))
                    pending.remove((due, s))
            if job in step_end:
                s = step_end[job]
                plan.append(("negmax", s))
                if job == len(jobs):
                    plan.append(("maxrows", s))
                else:
                    pending.append((job + 2, s))

    unit = quad = 0
    before = 0
    finish = []
    value = None
    for B in range(NB):
        quads = [(g, j) for g in range(G) for j in range(TPB * (B + 1))]
        for ql, (g, j) in enumerate(quads):
            lead = before + per_step[G * B] + LEAD
            rate = 2 + per_step[0] / len(quads)
            score_jobs(int(lead + ql * rate))
            for i in range(4):
                plan.append(("probs", unit, B, g, j, i))
                unit += 1
                if i == 0:
                    score_jobs(int(lead + (ql + 0.5) * rate))
                if i == 1 and value is not None:
                    plan.append(value)
                    if value[4] == TPB * (value[2] + 1) - 1:
                        plan.append(("keep", G * value[2] + value[3]))
            value = ("values", quad, B, g, j)
            quad += 1
            if ql >= 2 and finish:
                plan.append(finish.pop(0))
        before += len(quads) * 2
        assert not finish
        finish = [(k, TPB * B + t) for t in range(TPB) for k in ("heads_turn", "out_turn", "out_proj", "norm1")]
        if B == NB - 1:
            plan.append(value)
            plan.append(("keep", G * B + G - 1))
    return plan, finish


def block_kernel(nc, x, Wq, bq, Wk, bk, Wv, bv, Wo, bo, router_w, w_gate, w_up, w_down,
                 s_gate, s_up, s_down, out):
    _, T, D = x.shape
    H, HD = 16, 8
    G = H // 4
    NB, NT = T // BLK, T // P
    E, _, FF = w_gate.shape
    FC = FF // P
    NE = E + 1
    SCALE = float(HD) ** -0.5
    STACK = PARTS * PARTS * HD
    KROWS = 96
    VC = HD + 1
    assert D == P and H * HD == D and STACK + PARTS <= KROWS

    plan, tail = make_plan(NB, G)
    n_jobs = sum(1 for i in plan if i[0] == "scores")
    n_units = sum(1 for i in plan if i[0] == "probs")
    n_quads = sum(1 for i in plan if i[0] == "values")

    route0 = [("x_turn", 0), ("route", 0), ("xs_turn", 0)]
    first_q3 = [i for i, it in enumerate(plan) if it[0] == "values" and it[2] == NB - 1][NB * 4]
    later = [i for i, it in enumerate(plan) if it[0] == "values" and i > first_q3]
    for n, piece in enumerate(route0):
        plan.insert(later[20 + 3 * n] + n, piece)
    moe = []
    for b in range(NB):
        background = list(tail) if b == 0 else []
        route = [("x_turn", b + 1), ("route", b + 1), ("xs_turn", b + 1)] if b + 1 < NB else []
        for e in range(NE):
            moe.append(("hidden", b, e))
            if (b, e) != (0, 0):
                moe.append(("down", *((b, e - 1) if e else (b - 1, NE - 1))))
                if e == 0:
                    moe.append(("moments2", b - 1))
            if e == 1 and b:
                moe.append(("norm2", b - 1))
            for _ in range(2):
                if background:
                    moe.append(background.pop(0))
            if e in (3, 5, 7) and route:
                moe.append(route.pop(0))
    moe += [("down", NB - 1, NE - 1), ("moments2", NB - 1), ("norm2", NB - 1)]
    plan = plan + moe

    misc_kinds = ("maxrows", "heads_turn", "out_turn", "out_proj", "x_turn", "route", "xs_turn")
    misc_use = {it: n for n, it in enumerate(it for it in plan if it[0] in misc_kinds)}

    def upto(kind, item):
        return [it for it in plan if it[0] == kind].index(item) + 1

    ctx = ExitStack()
    with ctx:
        def sb(name, shape, dt):
            return ctx.enter_context(nc.sbuf_tensor(name, shape, dt))

        def sem(name):
            return ctx.enter_context(nc.semaphore(name))

        ident = sb("ident", [P, P], F32)
        ident_bf = sb("ident_bf", [P, P], BF16)
        mask_qk = sb("mask_qk", [P, P], BF16)
        mask_kq = sb("mask_kq", [P, P], BF16)
        x_sb = sb("x_sb", [P, NT, D], F32)
        xT = sb("xT", [P, 2, BLK], F32)
        wT = sb("wT", [P, 4, D], F32)
        r_nat = sb("r_nat", [E, D], F32)
        rT = sb("rT", [P, E], F32)
        bias_qk = sb("bias_qk", [P, 2], F32)
        bias_vo = sb("bias_vo", [P, 2, D], F32)
        qk_f = sb("qk_f", [P, 2, 2, BLK], F32)
        qk_parts = sb("qk_parts", [P, 2, 2, PARTS, BLK], BF16)
        q_stack = sb("q_stack", [P, 2, H, BLK], BF16)
        k_stack = sb("k_stack", [P, H, T], BF16)
        v_aug = sb("v_aug", [P, NT, H * VC + 32 - VC], F32)
        probs = sb("probs", [P, RING, BLK], F32)
        part_max = sb("part_max", [P, 2, TPB, 4, NB], F32)
        neg_max = sb("neg_max", [P, 2, TPB, 4], F32)
        max_parts = sb("max_parts", [P, 2, TPB, PARTS, 4], BF16)
        max_rows = sb("max_rows", [PARTS * 4, 2, BLK], BF16)
        oT = sb("oT", [P, 2, G, BLK], F32)
        w_nat = oT[:, 0, 0, :].rearrange("p (i d) -> p i d", i=4)
        denom_inv = sb("denom_inv", [P, H], F32)
        o_norm = sb("o_norm", [P, H, HD], F32)
        o_normT = sb("o_normT", [P, P], F32)
        y_res = sb("y_res", [P, D], F32)
        stats = sb("stats", [P, 6], F32)
        moments = sb("moments", [P, 2, TPB, 2], F32)
        rstd = sb("rstd", [P, 2, TPB], F32)
        minus_half = sb("minus_half", [P, TPB], F32)
        wg = sb("wg", [P, NE, FF], F32)
        wu = sb("wu", [P, NE, FF], F32)
        wd = sb("wd", [P, NE, FC, D], F32)
        x1T = xT
        xsT = qk_f[:, 0, :, :]
        xs = qk_f[:, 1, 0, :].rearrange("p (t d) -> p t d", t=TPB)
        logits = sb("logits", [P, TPB, E], F32)
        top = sb("top", [P, TPB], F32)
        best = sb("best", [P, TPB], F32)
        rank = sb("rank", [P, TPB, E], F32)
        order = sb("order", [P, E], F32)
        score = sb("score", [P, TPB], F32)
        half_hot = sb("half_hot", [P, 2, TPB, E], F32)
        after = q_stack[:, :, :, :].rearrange("p a h t -> p (a h t)").bitcast(F32)
        sig = after[:, 0:2 * BLK].rearrange("p (a n) -> p a n", a=2)
        hid = after[:, 2 * BLK:6 * BLK].rearrange("p (a n) -> p a n", a=4)
        acc = after[:, 6 * BLK:8 * BLK].rearrange("p (a t d) -> p a t d", a=2, t=TPB)
        y_out = after[:, 8 * BLK:10 * BLK].rearrange("p (a t d) -> p a t d", a=2, t=TPB)

        score_ps = ctx.enter_context(nc.psum_tensor("score_ps", [P, 2, 2, BLK], F32))
        prob_ps = ctx.enter_context(nc.psum_tensor("prob_ps", [P, 2, BLK], F32))
        out_ps = ctx.enter_context(nc.psum_tensor("out_ps", [P, BLK], F32))
        misc_ps = ctx.enter_context(nc.psum_tensor("misc_ps", [P, BLK], F32))

        x_loaded = [sem(f"x_loaded{b}") for b in range(NB)]
        proj_loaded = sem("proj_loaded")
        bias_loaded = sem("bias_loaded")
        moe_loaded = sem("moe_loaded")
        pool_step = sem("pool_step")
        k_filled = sem("k_filled")
        q_filled = sem("q_filled")
        consts_ready = sem("consts_ready")
        w_turned = sem("w_turned")
        w_kept = sem("w_kept")
        x_turned = sem("x_turned")
        x_kept = sem("x_kept")
        qk_made = sem("qk_made")
        qk_kept = sem("qk_kept")
        v_made = sem("v_made")
        v_kept = sem("v_kept")
        q_split = sem("q_split")
        k_split = sem("k_split")
        bo_added = sem("bo_added")
        q_stacked = [sem(f"q_stacked{b}") for b in range(NB)]
        k_stacked = [sem(f"k_stacked{b}") for b in range(NB)]
        dve_step = sem("dve_step")
        scores_ready = sem("scores_ready")
        scores_read = sem("scores_read")
        neg_max_ready = sem("neg_max_ready")
        max_turned = sem("max_turned")
        max_rows_kept = sem("max_rows_kept")
        max_rows_placed = [sem(f"max_rows_placed{i}") for i in range(2)]
        logits_ready = sem("logits_ready")
        exp_in_ready = sem("exp_in_ready")
        probs_ready = sem("probs_ready")
        values_done = sem("values_done")
        out_kept = sem("out_kept")
        heads_turned = sem("heads_turned")
        heads_normed = sem("heads_normed")
        out_turned = sem("out_turned")
        out_turn_kept = sem("out_turn_kept")
        out_projected = sem("out_projected")
        x1_ready = sem("x1_ready")
        y_made = sem("y_made")
        var1_ready = sem("var1_ready")
        rstd1_ready = sem("rstd1_ready")
        var2_ready = sem("var2_ready")
        rstd2_ready = sem("rstd2_ready")
        x1_turned = sem("x1_turned")
        x1T_kept = sem("x1T_kept")
        top_ready = sem("top_ready")
        score_tanh = sem("score_tanh")
        xs_ready = sem("xs_ready")
        xs_turned = sem("xs_turned")
        xsT_kept = sem("xsT_kept")
        hidden_made = sem("hidden_made")
        tanh_ready = sem("tanh_ready")
        hidden_ready = sem("hidden_ready")
        down_made = sem("down_made")
        down_added = sem("down_added")
        y_ready = sem("y_ready")
        y_stored = [sem(f"y_stored{i}") for i in range(2)]

        block = ctx.enter_context(nc.Block())

        x_tiles = x.rearrange("a (n p) d -> p (a n) d", p=P)
        out_tiles = out.rearrange("a (n p) d -> p (a n) d", p=P)

        STACKED = 16 * PARTS * PARTS
        CLEARED = 16

        units_before = {B: sum(1 for it in plan if it[0] == "probs" and it[2] < B) for B in range(NB + 1)}

        def last_quad(s):
            B, g = divmod(s, G)
            return next(it[1:] for it in plan if it[0] == "values" and it[2:] == (B, g, TPB * (B + 1) - 1))

        @block.sync
        def _(sp):
            for i, w in enumerate((Wq, Wk, Wv, Wo)):
                sp.dma_start(w_nat[:, i, :], w).then_inc(proj_loaded, 16)
            sp.dma_start(r_nat[:, :], router_w).then_inc(proj_loaded, 16)
            for b in range(1, NB):
                sp.dma_start(x_sb[:, TPB * b:TPB * b + TPB, :],
                             x_tiles[:, TPB * b:TPB * b + TPB, :]).then_inc(x_loaded[b], 16)

            def stack_k(b):
                sp.wait_ge(k_filled, b + 1)
                sp.wait_ge(k_split, b + 1)
                for r in range(PARTS):
                    for a in range(PARTS):
                        row = (r * PARTS + a) * HD
                        for_head = k_stack[row:row + HD, :, b * BLK:(b + 1) * BLK]
                        src = qk_parts[:, 1, b % 2, r, :]
                        sp.dma_start(for_head, src).then_inc(k_stacked[b], 16)

            def stack_q(b):
                sp.wait_ge(q_filled, min(b, 1) + 1)
                sp.wait_ge(q_split, b + 1)
                if b >= 2:
                    sp.wait_ge(exp_in_ready, units_before[b - 1])
                    sp.dma_start(q_stack[STACK:STACK + PARTS, b % 2, :, :],
                                 q_stack[STACK + PARTS:STACK + 2 * PARTS, b % 2, :, :]).then_inc(q_stacked[b], 16)
                for r in range(PARTS):
                    for a in range(PARTS):
                        row = (r * PARTS + a) * HD
                        for_head = q_stack[row:row + HD, b % 2, :, :]
                        src = qk_parts[:, 0, b % 2, a, :]
                        sp.dma_start(for_head, src).then_inc(q_stacked[b], 16)

            for b in range(NB):
                if b < 2:
                    stack_q(b)
                stack_k(b)
            for w, s, dst in ((w_gate, s_gate, wg), (w_up, s_up, wu)):
                sp.dma_start(dst[:, 0:E, :], w.rearrange("e d f -> d e f")).then_inc(moe_loaded, 16)
                sp.dma_start(dst[:, E, :], s).then_inc(moe_loaded, 16)
            for e in range(E):
                sp.dma_start(wd[:, e, :, :], w_down[e].rearrange("(c p) d -> p c d", p=P)).then_inc(moe_loaded, 16)
            sp.dma_start(wd[:, E, :, :], s_down.rearrange("(c p) d -> p c d", p=P)).then_inc(moe_loaded, 16)
            for s in range(NB * G):
                if s in (5, 9):
                    stack_q(s // 4 + 1)
                B, g = divmod(s, G)
                sp.wait_ge(max_rows_kept, s + 1)
                for a in range(PARTS):
                    sp.dma_start(q_stack[STACK + a:STACK + a + 1, B % 2, 4 * g:4 * g + 4, :],
                                 max_rows[4 * a:4 * a + 4, s % 2, :]).then_inc(max_rows_placed[s % 2], 16)
            for b in range(NB):
                sp.wait_ge(y_ready, b + 1)
                sp.dma_start(out_tiles[:, TPB * b:TPB * b + TPB, :], y_out[:, b % 2]).then_inc(y_stored[b % 2], 16)
            for i in range(2):
                sp.wait_ge(y_stored[i], 16 * NB // 2)

        @block.gpsimd
        def _(pool):
            pool.memset(ident[:, :], 0.0).then_inc(pool_step, 1)
            pool.memset(mask_qk[:, :], 0.0).then_inc(pool_step, 1)
            pool.wait_ge(pool_step, 2)
            pool.affine_select(out=ident[:, :], in_=ident[:, :], compare_op=ALU.not_equal, fill=1.0,
                               base=0, pattern=[[-1, P]], channel_multiplier=1).then_inc(pool_step, 1)
            pool.affine_select(out=mask_kq[:, :], in_=mask_qk[:, :], compare_op=ALU.is_ge, fill=MASKED,
                               base=0, pattern=[[1, P]], channel_multiplier=-1).then_inc(pool_step, 1)
            pool.wait_ge(pool_step, 4)
            pool.tensor_copy(ident_bf[:, :], ident[:, :]).then_inc(pool_step, 1)
            pool.affine_select(out=mask_qk[:, :], in_=mask_qk[:, :], compare_op=ALU.is_ge, fill=MASKED,
                               base=0, pattern=[[-1, P]], channel_multiplier=1).then_inc(pool_step, 1)
            pool.wait_ge(pool_step, 6)
            for b in range(NB):
                ones_pair = k_stack[64:96, :, b * BLK:(b + 1) * BLK].bitcast(F32)
                pool.memset(ones_pair, ONES_PAIR).then_inc(k_filled, 1)
                pool.wait_ge(k_filled, b + 1)
            pool.memset(v_aug[:, :, :], 1.0).then_inc(consts_ready, 1)
            for e in range(E):
                pool.memset(order[:, e:e + 1], float(E - e)).then_inc(consts_ready, 1)
            steps = 6
            for b in range(NB):
                pool.wait_ge(qk_kept, 2 * b + 2)
                if b >= 2:
                    pool.wait_ge(k_stacked[b - 2], STACKED)
                rest = qk_f[:, 1, b % 2, :]
                for a in range(PARTS):
                    part = qk_parts[:, 1, b % 2, a, :]
                    copied = pool.tensor_copy(part, rest)
                    if a == PARTS - 1:
                        copied.then_inc(k_split, 1)
                        break
                    copied.then_inc(pool_step, 1)
                    steps += 1
                    pool.wait_ge(pool_step, steps)
                    pool.tensor_tensor(rest, rest, part, ALU.subtract).then_inc(pool_step, 1)
                    steps += 1
                    pool.wait_ge(pool_step, steps)
            pool.memset(minus_half[:, :], -0.5).then_inc(pool_step, 1)
            steps += 1
            pool.wait_ge(pool_step, steps)
            pool.wait_ge(bias_loaded, 64)
            for b in range(NB):
                pool.wait_ge(x_turned, b + 1)
                here = x_sb[:, TPB * b:TPB * b + TPB, :]
                pool.tensor_tensor(here, here, bias_vo[:, 1:2, :].to_broadcast([P, TPB, D]),
                                   ALU.add).then_inc(bo_added, 1)
            for it in plan:
                kind = it[0]
                if kind == "out_proj":
                    T0 = it[1]
                    pool.wait_ge(var1_ready, T0 + 1)
                    pool.tensor_tensor(rstd[:, 0, T0 % TPB:T0 % TPB + 1], rstd[:, 0, T0 % TPB:T0 % TPB + 1],
                                       minus_half[:, 0:1], ALU.pow).then_inc(rstd1_ready, 1)
                elif kind == "moments2":
                    pool.wait_ge(var2_ready, it[1] + 1)
                    pool.tensor_tensor(rstd[:, 1, :], rstd[:, 1, :], minus_half[:, :], ALU.pow).then_inc(rstd2_ready, 1)

        @block.scalar
        def _(act):
            act.dma_start(x_sb[:, 0:TPB, :], x_tiles[:, 0:TPB, :]).then_inc(x_loaded[0], 16)
            for i, bias in enumerate((bq, bk)):
                act.dma_start(bias_qk[:, i:i + 1], bias.rearrange("(h d) -> d h", d=HD),
                              allow_slow_non_contiguous=True).then_inc(bias_loaded, 16)
            for i, bias in enumerate((bv, bo)):
                act.dma_start(bias_vo[:, i, :], bias.rearrange("(a d) -> a d", a=1).to_broadcast([P, D])
                              ).then_inc(bias_loaded, 16)
            act.wait_ge(w_turned, 1)
            for i in range(2):
                act.activation(wT[:, i, :].rearrange("p (d h) -> p d h", d=HD),
                               misc_ps[:, i * D:(i + 1) * D].rearrange("p (h d) -> p d h", d=HD), ACT.Copy).then_inc(w_kept, 1)
            act.activation(wT[:, 2:4, :], misc_ps[:, 2 * D:4 * D].rearrange("p (i d) -> p i d", i=2), ACT.Copy).then_inc(w_kept, 1)
            act.wait_ge(w_turned, 2)
            act.activation(rT[:, :], misc_ps[:, 0:E], ACT.Copy).then_inc(w_kept, 1)
            act.wait_ge(bias_loaded, 64)
            for b in range(NB):
                act.wait_ge(x_turned, b + 1)
                if b >= 2:
                    act.wait_ge(v_made, b - 1)
                act.activation(xT[:, b % 2, :], score_ps[:, 0, 0, :], ACT.Copy).then_inc(x_kept, 1)
                for side in range(2):
                    act.wait_ge(qk_made, 2 * b + side + 1)
                    if b >= 2:
                        act.wait_ge((q_split, k_split)[side], b - 1)
                    act.activation(qk_f[:, side, b % 2, :], prob_ps[:, side, :], ACT.Identity,
                                   bias=bias_qk[:, side:side + 1]).then_inc(qk_kept, 1)

            for it in plan:
                kind = it[0]
                if kind == "probs":
                    _, n, B, g, j, i = it
                    w = BLK - P * max(0, j - TPB * B)
                    act.wait_ge(exp_in_ready, n + 1)
                    if n >= RING:
                        act.wait_ge(values_done, (n - RING) // 4 + 1)
                    act.activation(probs[:, n % RING, 0:w], prob_ps[:, n % 2, 0:w], ACT.Exp,
                                   scale=SCALE).then_inc(probs_ready, 1)
                elif kind == "maxrows":
                    s = it[1]
                    act.wait_ge(max_turned, s + 1)
                    if s >= 2:
                        act.wait_ge(max_rows_placed[s % 2], 16 * PARTS * (s // 2))
                    act.activation(max_rows[:, s % 2, :], misc_ps[0:4 * PARTS, :], ACT.Copy).then_inc(max_rows_kept, 1)
                elif kind == "keep":
                    s = it[1]
                    B, g = divmod(s, G)
                    act.wait_ge(values_done, upto("values", ("values", *last_quad(s))))
                    if B >= 2:
                        act.wait_ge(heads_turned, TPB * (B - 1))
                    act.activation(oT[:, B % 2, g, :], out_ps[:, :], ACT.Copy).then_inc(out_kept, 1)
                elif kind == "out_turn":
                    act.wait_ge(out_turned, it[1] + 1)
                    if it[1] >= 1:
                        act.wait_ge(out_projected, it[1])
                    act.activation(o_normT[:, :], misc_ps[:, 0:P], ACT.Copy).then_inc(out_turn_kept, 1)
                elif kind == "x_turn":
                    b = it[1]
                    act.wait_ge(x1_turned, b + 1)
                    if b >= 2:
                        act.wait_ge(hidden_made, (b - 1) * NE * FC)
                    act.activation(x1T[:, b % 2, :], misc_ps[:, :], ACT.Copy).then_inc(x1T_kept, 1)
                elif kind == "route":
                    b = it[1]
                    act.wait_ge(top_ready, b + 1)
                    act.activation(score[:, :], top[:, :], ACT.Tanh, scale=0.5).then_inc(score_tanh, 1)
                elif kind == "xs_turn":
                    b = it[1]
                    act.wait_ge(xs_turned, b + 1)
                    if b >= 2:
                        act.wait_ge(hidden_made, (b - 1) * NE * FC)
                    act.activation(xsT[:, b % 2, :], misc_ps[:, :], ACT.Copy).then_inc(xsT_kept, 1)
                elif kind == "hidden":
                    _, b, e = it
                    for f in range(FC):
                        r = (b * NE + e) * FC + f
                        act.wait_ge(hidden_made, r + 1)
                        if r >= 2:
                            act.wait_ge(hidden_ready, r - 1)
                        act.activation(sig[:, r % 2, :], score_ps[:, r % 2, 0, :], ACT.Tanh,
                                       scale=0.5).then_inc(tanh_ready, 1)

        @block.vector
        def _(dve):
            chain = [0]

            def link(ins):
                chain[0] += 1
                ins.then_inc(dve_step, 1)
                dve.wait_ge(dve_step, chain[0])

            def moments_of(which, t, src):
                link(dve.bn_stats(stats[:, :], src))
                link(dve.bn_aggr(moments[:, which, t, :], stats[:, :]))
                return dve.tensor_scalar(rstd[:, which, t:t + 1], moments[:, which, t, 1:2], LN_EPS, None, ALU.add)

            def normalised(which, t, dst, src):
                return dve.tensor_scalar(dst, src, moments[:, which, t, 0:1], rstd[:, which, t:t + 1],
                                         ALU.subtract, ALU.mult)

            for slot in range(2):
                dve.memset(q_stack[64:96, slot, :, :].bitcast(F32), 0.0).then_inc(q_filled, 1)
            dve.wait_ge(bias_loaded, 64)
            for b in range(NB):
                dve.wait_ge(qk_kept, 2 * b + 1)
                rest = qk_f[:, 0, b % 2, :]
                if b >= 2:
                    dve.wait_ge(q_stacked[b - 2], STACKED)
                for a in range(PARTS):
                    part = qk_parts[:, 0, b % 2, a, :]
                    copied = dve.tensor_copy(part, rest)
                    if a == PARTS - 1:
                        copied.then_inc(q_split, 1)
                        break
                    link(copied)
                    link(dve.tensor_tensor(rest, rest, part, ALU.subtract))
                dve.wait_ge(consts_ready, 1)
                dve.wait_ge(v_made, b + 1)
                for t in range(TPB):
                    dst = v_aug[:, TPB * b + t, 0:H * VC].rearrange("p (h c) -> p h c", c=VC)[:, :, 0:HD]
                    last = dve.tensor_tensor(dst, score_ps[:, 1, 0, t * P:(t + 1) * P].rearrange("p (h c) -> p h c", c=HD),
                                             bias_vo[:, 0, :].rearrange("p (h c) -> p h c", c=HD), ALU.add)
                last.then_inc(v_kept, 1)

            for it in plan:
                kind = it[0]
                if kind == "scores":
                    _, m, B, g, t, c, hp = it
                    w = min(BLK, P * (TPB * B + t + 1) - BLK * c)
                    s = G * B + g
                    dve.wait_ge(scores_ready, m + 1)
                    dve.tensor_reduce(out=part_max[:, s % 2, t, 2 * hp:2 * hp + 2, c], in_=score_ps[:, m % 2, :, 0:w],
                                      axis=AX.X, op=ALU.max).then_inc(scores_read, 1)
                elif kind == "negmax":
                    s = it[1]
                    B = s // G
                    dve.wait_ge(scores_read, sum(2 * TPB * (q // G + 1) for q in range(s + 1)))
                    if s >= 2:
                        dve.wait_ge(max_turned, s - 1)
                    rest = neg_max[:, s % 2, :, :]
                    link(dve.tensor_reduce(out=rest, in_=part_max[:, s % 2, :, :, 0:B + 1],
                                           axis=AX.X, op=ALU.max, negate=True))
                    for a in range(PARTS):
                        part = max_parts[:, s % 2, :, a, :]
                        copied = dve.tensor_copy(part, rest)
                        if a == PARTS - 1:
                            copied.then_inc(neg_max_ready, 1)
                            break
                        link(copied)
                        link(dve.tensor_tensor(rest, rest, part, ALU.subtract))
                elif kind == "heads_turn":
                    T0 = it[1]
                    dve.wait_ge(heads_turned, T0 + 1)
                    by_head = misc_ps[:, :].rearrange("p (h c) -> p h c", c=32)
                    link(dve.reciprocal(denom_inv[:, :], by_head[:, :, HD]))
                    if T0 >= 1:
                        dve.wait_ge(out_turned, T0)
                    dve.tensor_tensor(o_norm[:, :, :], by_head[:, :, 0:HD],
                                      denom_inv[:, :].rearrange("p (h c) -> p h c", c=1).to_broadcast([P, H, HD]),
                                      ALU.mult).then_inc(heads_normed, 1)
                elif kind == "out_proj":
                    T0 = it[1]
                    dve.wait_ge(out_projected, T0 + 1)
                    dve.wait_ge(bo_added, T0 // TPB + 1)
                    dve.tensor_tensor(y_res[:, :], misc_ps[:, 0:D], x_sb[:, T0, :], ALU.add).then_inc(y_made, 1)
                    dve.wait_ge(y_made, T0 + 1)
                    moments_of(0, T0 % TPB, y_res[:, :]).then_inc(var1_ready, 1)
                elif kind == "norm1":
                    T0 = it[1]
                    dve.wait_ge(rstd1_ready, T0 + 1)
                    normalised(0, T0 % TPB, x_sb[:, T0, :], y_res[:, :]).then_inc(x1_ready, 1)
                    dve.wait_ge(x1_ready, T0 + 1)
                elif kind == "route":
                    b = it[1]
                    dve.wait_ge(logits_ready, b + 1)
                    link(dve.tensor_copy(logits[:, :, :], misc_ps[:, 0:TPB * E].rearrange("p (t e) -> p t e", e=E)))
                    if b >= 1:
                        dve.wait_ge(xs_ready, b)
                    dve.tensor_reduce(out=top[:, :], in_=logits[:, :, :], axis=AX.X, op=ALU.max).then_inc(top_ready, 1)
                    dve.wait_ge(top_ready, b + 1)
                    spread = lambda v: v.rearrange("p (t a) -> p t a", a=1).to_broadcast([P, TPB, E])
                    link(dve.tensor_tensor(rank[:, :, :], logits[:, :, :], spread(top[:, :]), ALU.is_equal))
                    if b == 0:
                        dve.wait_ge(consts_ready, 1 + E)
                    link(dve.tensor_tensor(rank[:, :, :], rank[:, :, :],
                                           order[:, :].rearrange("p (a e) -> p a e", a=1).to_broadcast([P, TPB, E]), ALU.mult))
                    link(dve.tensor_reduce(out=best[:, :], in_=rank[:, :, :], axis=AX.X, op=ALU.max))
                    link(dve.tensor_tensor(rank[:, :, :], rank[:, :, :], spread(best[:, :]), ALU.is_equal))
                    if b >= 2:
                        dve.wait_ge(down_added, (b - 1) * NE)
                    link(dve.tensor_scalar(half_hot[:, b % 2, :, :], rank[:, :, :], 0.5, None, ALU.mult))
                    dve.wait_ge(score_tanh, b + 1)
                    if b >= 1:
                        dve.wait_ge(xs_turned, b)
                    link(dve.tensor_scalar(score[:, :], score[:, :], 0.5, 0.5, ALU.mult, ALU.add))
                    for t in range(TPB):
                        last = dve.tensor_scalar(xs[:, t, :], x_sb[:, TPB * b + t, :], score[:, t:t + 1], None, ALU.mult)
                    last.then_inc(xs_ready, 1)
                elif kind == "hidden":
                    _, b, e = it
                    for f in range(FC):
                        r = (b * NE + e) * FC + f
                        dve.wait_ge(tanh_ready, r + 1)
                        link(dve.scalar_tensor_tensor(out=sig[:, r % 2, :], in0=sig[:, r % 2, :], scalar=1.0,
                                                      in1=score_ps[:, r % 2, 0, :], op0=ALU.add, op1=ALU.mult))
                        if r >= 2 * FC:
                            dve.wait_ge(down_made, r // FC - 1)
                        dve.tensor_tensor(hid[:, r % 4, :], sig[:, r % 2, :], score_ps[:, r % 2, 1, :],
                                          ALU.mult).then_inc(hidden_ready, 1)
                elif kind == "down":
                    _, b, e = it
                    n = b * NE + e
                    dve.wait_ge(down_made, n + 1)
                    if n >= 1:
                        dve.wait_ge(down_added, n)
                    if e < E:
                        for t in range(TPB):
                            so_far = x_sb[:, TPB * b + t, :] if e == 0 else acc[:, b % 2, t, :]
                            last = dve.scalar_tensor_tensor(
                                out=acc[:, b % 2, t, :], in0=prob_ps[:, n % 2, t * P:(t + 1) * P],
                                scalar=half_hot[:, b % 2, t, e:e + 1], in1=so_far, op0=ALU.mult, op1=ALU.add)
                    else:
                        last = dve.scalar_tensor_tensor(
                            out=acc[:, b % 2, :, :].rearrange("p t d -> p (t d)"), in0=prob_ps[:, n % 2, :], scalar=0.5,
                            in1=acc[:, b % 2, :, :].rearrange("p t d -> p (t d)"), op0=ALU.mult, op1=ALU.add)
                    last.then_inc(down_added, 1)
                elif kind == "moments2":
                    b = it[1]
                    dve.wait_ge(down_added, (b + 1) * NE)
                    for t in range(TPB):
                        made = moments_of(1, t, acc[:, b % 2, t, :])
                        if t < TPB - 1:
                            link(made)
                    made.then_inc(var2_ready, 1)
                elif kind == "norm2":
                    b = it[1]
                    dve.wait_ge(rstd2_ready, b + 1)
                    if b >= 2:
                        dve.wait_ge(y_stored[b % 2], 16 * (b // 2))
                    for t in range(TPB):
                        last = normalised(1, t, y_out[:, b % 2, t, :], acc[:, b % 2, t, :])
                    last.then_inc(y_ready, 1)

        @block.tensor
        def _(pe):
            mm, turn = pe.matmul, pe.transpose

            pe.wait_ge(pool_step, 6)
            pe.wait_ge(proj_loaded, 16 * 5)
            for i in range(4):
                last = turn(misc_ps[:, i * P:(i + 1) * P], w_nat[:, i, :], ident[:, :])
            last.then_inc(w_turned, 1)
            pe.wait_ge(w_kept, 3)
            turn(misc_ps[:, 0:E], r_nat[:, :], ident[0:E, 0:E]).then_inc(w_turned, 1)
            for b in range(NB):
                pe.wait_ge(x_loaded[b], 16)
                if b >= 1:
                    pe.wait_ge(x_kept, b)
                for t in range(TPB):
                    last = turn(score_ps[:, 0, 0, t * P:(t + 1) * P], x_sb[:, TPB * b + t, :], ident[:, :])
                last.then_inc(x_turned, 1)
                pe.wait_ge(x_kept, b + 1)
                for side in range(2):
                    if b >= 1:
                        pe.wait_ge(qk_kept, 2 * b - 1 + side)
                    mm(prob_ps[:, side, :], wT[:, side, :], xT[:, b % 2, :], start=True, stop=True).then_inc(qk_made, 1)
                if b >= 1:
                    pe.wait_ge(v_kept, b)
                for t in range(TPB):
                    last = mm(score_ps[:, 1, 0, t * P:(t + 1) * P], xT[:, b % 2, t * P:(t + 1) * P], wT[:, 2, :],
                              start=True, stop=True)
                last.then_inc(v_made, 1)

            pe.wait_ge(x_kept, NB)
            pe.wait_ge(qk_kept, 2 * NB)
            pe.wait_ge(v_kept, NB)
            pe.wait_ge(w_kept, 4)

            def free_misc(it):
                u = misc_use[it]
                if not u:
                    return
                before = [k for k, v in misc_use.items() if v == u - 1][0]
                kind, i = before
                read = {"maxrows": max_rows_kept, "heads_turn": heads_normed, "out_turn": out_turn_kept,
                        "out_proj": y_made, "x_turn": x1T_kept, "route": top_ready, "xs_turn": xsT_kept}[kind]
                pe.wait_ge(read, i + 1)

            for it in plan:
                kind = it[0]
                if kind == "scores":
                    _, m, B, g, t, c, hp = it
                    T0 = TPB * B + t
                    w = min(BLK, P * (T0 + 1) - BLK * c)
                    if m >= 2:
                        pe.wait_ge(scores_read, m - 1)
                    if g == 0 and t == 0:
                        pe.wait_ge(k_stacked[c], STACKED)
                        pe.wait_ge(q_stacked[B], STACKED + (CLEARED if B >= 2 else 0))
                    for i in range(2):
                        h = 4 * g + 2 * hp + i
                        last = mm(score_ps[:, m % 2, i, 0:w], q_stack[0:KROWS, B % 2, h, t * P:(t + 1) * P],
                                  k_stack[0:KROWS, h, c * BLK:c * BLK + w], start=True, stop=c < B)
                        if c == B:
                            last = mm(score_ps[:, m % 2, i, w - P:w], ident_bf[:, :], mask_qk[:, :],
                                      start=False, stop=True)
                    last.then_inc(scores_ready, 1)
                elif kind == "maxrows":
                    s = it[1]
                    free_misc(it)
                    pe.wait_ge(neg_max_ready, s + 1)
                    for t in range(TPB):
                        last = mm(misc_ps[0:4 * PARTS, t * P:(t + 1) * P],
                                  max_parts[:, s % 2, t, :, :].rearrange("p a h -> p (a h)"), ident_bf[:, :],
                                  start=True, stop=True)
                    last.then_inc(max_turned, 1)
                elif kind == "probs":
                    _, n, B, g, j, i = it
                    s = G * B + g
                    skip = P * max(0, j - TPB * B)
                    w = BLK - skip
                    h = 4 * g + i
                    if n >= 2:
                        pe.wait_ge(probs_ready, n - 1)
                    if j == 0 and i == 0:
                        pe.wait_ge(max_rows_placed[s % 2], 16 * PARTS * (s // 2 + 1))
                    diagonal = j >= TPB * B
                    last = mm(prob_ps[:, n % 2, 0:w], k_stack[0:KROWS, h, j * P:(j + 1) * P],
                              q_stack[0:KROWS, B % 2, h, skip:BLK], start=True, stop=not diagonal)
                    if diagonal:
                        last = mm(prob_ps[:, n % 2, 0:P], ident_bf[:, :], mask_kq[:, :], start=False, stop=True)
                    last.then_inc(exp_in_ready, 1)
                elif kind == "values":
                    _, k, B, g, j = it
                    s = G * B + g
                    skip = P * max(0, j - TPB * B)
                    w = BLK - skip
                    pe.wait_ge(probs_ready, 4 * k + 4)
                    if j == 0 and s >= 1:
                        pe.wait_ge(out_kept, s)
                    for i in range(4):
                        h = 4 * g + i
                        last = mm(out_ps[32 * i:32 * i + 32, skip:BLK], v_aug[:, j, h * VC:h * VC + 32],
                                  probs[:, (4 * k + i) % RING, 0:w], start=j == 0, stop=j == TPB * (B + 1) - 1)
                    last.then_inc(values_done, 1)
                elif kind == "heads_turn":
                    T0 = it[1]
                    B, t = divmod(T0, TPB)
                    free_misc(it)
                    pe.wait_ge(out_kept, G * (B + 1))
                    for g in range(G):
                        last = turn(misc_ps[:, g * P:(g + 1) * P], oT[:, B % 2, g, t * P:(t + 1) * P], ident[:, :])
                    last.then_inc(heads_turned, 1)
                elif kind == "out_turn":
                    free_misc(it)
                    pe.wait_ge(heads_normed, it[1] + 1)
                    turn(misc_ps[:, 0:P], o_norm[:, :, :].rearrange("p h c -> p (h c)"), ident[:, :]).then_inc(out_turned, 1)
                elif kind == "out_proj":
                    free_misc(it)
                    pe.wait_ge(out_turn_kept, it[1] + 1)
                    mm(misc_ps[:, 0:D], o_normT[:, :], wT[:, 3, :], start=True, stop=True).then_inc(out_projected, 1)
                elif kind == "x_turn":
                    b = it[1]
                    free_misc(it)
                    pe.wait_ge(x1_ready, TPB * (b + 1))
                    for t in range(TPB):
                        last = turn(misc_ps[:, t * P:(t + 1) * P], x_sb[:, TPB * b + t, :], ident[:, :])
                    last.then_inc(x1_turned, 1)
                elif kind == "route":
                    b = it[1]
                    free_misc(it)
                    pe.wait_ge(x1T_kept, b + 1)
                    for t in range(TPB):
                        last = mm(misc_ps[:, t * E:(t + 1) * E], x1T[:, b % 2, t * P:(t + 1) * P], rT[:, :],
                                  start=True, stop=True)
                    last.then_inc(logits_ready, 1)
                elif kind == "xs_turn":
                    b = it[1]
                    free_misc(it)
                    pe.wait_ge(xs_ready, b + 1)
                    for t in range(TPB):
                        last = turn(misc_ps[:, t * P:(t + 1) * P], xs[:, t, :], ident[:, :])
                    last.then_inc(xs_turned, 1)
                elif kind == "hidden":
                    _, b, e = it
                    if (b, e) == (0, 0):
                        pe.wait_ge(moe_loaded, 16 * (4 + NE))
                        pe.wait_ge(scores_read, n_jobs)
                    if e == 0:
                        pe.wait_ge(xsT_kept, b + 1)
                    tokens = x1T if e == E else xsT
                    for f in range(FC):
                        r = (b * NE + e) * FC + f
                        if r >= 2:
                            pe.wait_ge(hidden_ready, r - 1)
                        mm(score_ps[:, r % 2, 0, :], wg[:, e, f * P:(f + 1) * P], tokens[:, b % 2, :], start=True, stop=True)
                        mm(score_ps[:, r % 2, 1, :], wu[:, e, f * P:(f + 1) * P], tokens[:, b % 2, :],
                           start=True, stop=True).then_inc(hidden_made, 1)
                elif kind == "down":
                    _, b, e = it
                    n = b * NE + e
                    pe.wait_ge(hidden_ready, FC * (n + 1))
                    if n >= 2:
                        pe.wait_ge(down_added, n - 1)
                    else:
                        pe.wait_ge(probs_ready, n_units)
                    for t in range(TPB):
                        for f in range(FC):
                            last = mm(prob_ps[:, n % 2, t * P:(t + 1) * P], hid[:, (FC * n + f) % 4, t * P:(t + 1) * P],
                                      wd[:, e, f, :], start=f == 0, stop=f == FC - 1)
                    last.then_inc(down_made, 1)


_INS = ['L0_attn_x', 'L0_attn_Wq', 'L0_attn_bq', 'L0_attn_Wk', 'L0_attn_bk', 'L0_attn_Wv', 'L0_attn_bv',
        'L0_attn_Wo', 'L0_attn_bo', 'L0_ffn_router_w', 'L0_ffn_expert_gate', 'L0_ffn_expert_up',
        'L0_ffn_expert_down', 'L0_ffn_shared_gate', 'L0_ffn_shared_up', 'L0_ffn_shared_down']
_OUTS = [((1, 2048, 128), 'float32')]


def kernel(**inputs):
    import numpy as _np
    import concourse.bacc as _bacc
    from concourse import mybir as _mybir
    from concourse.bass_utils import run_bass_kernel_spmd as _run

    nc = _bacc.Bacc("TRN2", target_bir_lowering=False, num_devices=1)
    arrays, args = {}, []
    for name in _INS:
        a = _np.ascontiguousarray(inputs[name])
        arrays[f"in_{name}_dram"] = a
        args.append(nc.dram_tensor(f"in_{name}_dram", a.shape, _mybir.dt.from_np(a.dtype), kind="ExternalInput").ap())
    for i, (shape, dtype) in enumerate(_OUTS):
        dt = _mybir.dt.from_np(_np.dtype(dtype))
        args.append(nc.dram_tensor(f"out_{i}_dram", shape, dt, kind="ExternalOutput").ap())
    block_kernel(nc, *args)
    r = _run(nc, [arrays], core_ids=[0])
    got = tuple(r.results[0][f"out_{i}_dram"] for i in range(len(_OUTS)))
    return got[0]
```

```python
import struct
from contextlib import ExitStack

import concourse.bass as bass
from concourse import mybir

F32 = mybir.dt.float32
BF16 = mybir.dt.bfloat16
F16 = mybir.dt.float16
I32 = mybir.dt.int32
ALU = mybir.AluOpType
ACT = mybir.ActivationFunctionType
AX = mybir.AxisListType

P = 128
BLK = 512
TPB = BLK // P
MASKED = -1.0e30
ONES_PAIR = struct.unpack('<f', bytes.fromhex('803f803f'))[0]
LN_EPS = 1e-5
PARTS = 3
LEAD = 8
BANKS = 3
PREPARE = ("x_in", "q_in", "k_in", "v_in")
START = (0, 2, 2, 2)
BACKLOG = 600
HOLD = 2
VECTOR_JOB = 1.9
VALUE_LAG = 3
RING = 8


def make_plan(NB, G):
    tensor_ns = {"x_in": 436, "q_in": 858, "k_in": 858, "v_in": 872, "heads_turn": 436, "out_turn": 109,
                 "out_proj": 218, "norm1": 0, "maxrows": 212, "negmax": 0, "keep": 0}
    vector_ns = {"q_in": 2900, "k_in": 2900, "v_in": 900, "heads_turn": 600, "out_proj": 1000, "norm1": 250,
                 "negmax": 1200}
    clock = {"tensor": 0.0, "vector": 0.0}
    jobs = [(B, g, t, c, hp) for B in range(NB) for g in range(G) for t in range(TPB)
            for c in range(B + 1) for hp in range(2)]
    per_step = [2 * TPB * (B + 1) for B in range(NB) for g in range(G)]
    step_end, at = {}, 0
    for s, n in enumerate(per_step):
        at += n
        step_end[at] = s
    plan, job, pending = [], 0, []

    def put(item, tensor=None, vector=None):
        plan.append(item)
        clock["tensor"] += tensor_ns[item[0]] if tensor is None else tensor
        spent = vector_ns.get(item[0], 0) if vector is None else vector
        if spent:
            clock["vector"] = max(clock["vector"], clock["tensor"]) + spent

    def score_jobs(upto):
        nonlocal job
        while job < min(upto, len(jobs)):
            if clock["vector"] - clock["tensor"] > BACKLOG and job > upto - HOLD:
                return
            B, g, t, c, hp = jobs[job]
            w = min(BLK, P * (TPB * B + t + 1) - BLK * c)
            put(("scores", job, *jobs[job]), tensor=0.84 * w + 107 * (c == B), vector=VECTOR_JOB * w)
            job += 1
            for due, s in list(pending):
                if job >= due or job == len(jobs):
                    put(("maxrows", s))
                    pending.remove((due, s))
            if job in step_end:
                s = step_end[job]
                put(("negmax", s))
                if job == len(jobs):
                    put(("maxrows", s))
                else:
                    pending.append((job + 2, s))

    for kind in PREPARE:
        put((kind, 0))
    unit = quad = 0
    before = 0
    finish = []
    value = None
    for B in range(NB):
        background = [(k, B + 1) for k in PREPARE if B + 1 < NB] + finish
        quads = [(g, j) for g in range(G) for j in range(TPB * (B + 1))]
        for ql, (g, j) in enumerate(quads):
            lead = before + per_step[G * B] + LEAD
            rate = 2 + per_step[0] / len(quads)
            w = BLK - P * max(0, j - TPB * B)
            score_jobs(int(lead + ql * rate))
            for i in range(4):
                put(("probs", unit, B, g, j, i), tensor=0.42 * w)
                unit += 1
                score_jobs(int(lead + (ql + (i + 1) / 4) * rate))
                if i == VALUE_LAG and value is not None:
                    put(value, tensor=936)
                    if value[4] == TPB * (value[2] + 1) - 1:
                        put(("keep", G * value[2] + value[3]))
            value = ("values", quad, B, g, j)
            quad += 1
            if ql >= START[B] and background:
                put(background.pop(0))
                if B == 0 and background:
                    put(background.pop(0))
        before += len(quads) * 2
        assert not background
        finish = [(k, TPB * B + t) for t in range(TPB) for k in ("heads_turn", "out_turn", "out_proj", "norm1")]
    put(value, tensor=936)
    put(("keep", G * B + G - 1))
    return plan, finish


def block_kernel(nc, x, Wq, bq, Wk, bk, Wv, bv, Wo, bo, router_w, w_gate, w_up, w_down,
                 s_gate, s_up, s_down, out):
    _, T, D = x.shape
    H, HD = 16, 8
    G = H // 4
    NB, NT = T // BLK, T // P
    E, _, FF = w_gate.shape
    FC = FF // P
    NE = E + 1
    NX = (T + E * (P - 1)) // P
    SCALE = float(HD) ** -0.5
    STACK = PARTS * PARTS * HD
    KROWS = 96
    VC = HD + 1
    assert D == P and H * HD == D and STACK + PARTS <= KROWS

    plan, tail = make_plan(NB, G)
    n_jobs = sum(1 for i in plan if i[0] == "scores")
    n_units = sum(1 for i in plan if i[0] == "probs")
    n_quads = sum(1 for i in plan if i[0] == "values")

    first = [i for i, it in enumerate(plan) if it[0] == "values" and it[2] == NB - 1]
    for n, piece in enumerate((k, b) for b in range(NB - 1) for k in ("x_turn", "route")):
        plan.insert(first[-14 + 2 * n] + n, piece)
    shared = [(k, b, *f) for b in range(NB) for k, f in (("shared", (0,)), ("shared", (1,)), ("shared_out", ()))]
    moe = []
    for piece in tail:
        moe += [piece] + ([shared.pop(0)] if piece[0] != "norm1" and len(shared) > 5 else [])
    for piece in (("x_turn", NB - 1), ("route", NB - 1), ("positions",), ("order",)):
        moe += [piece] + [shared.pop(0)]
        if piece[0] == "route":
            moe += [shared.pop(0)]
    assert len(shared) == 0, shared
    for k in range(-3, NX + 1):
        for kind, lag in (("sorted_in", 3), ("gate_up", 2), ("hid_turn", 0), ("expert_out", -1)):
            if 0 <= k + lag < NX:
                moe.append((kind, k + lag))
    for b in range(NB):
        moe += [("moments2", b), ("norm2", b)]
    plan = plan + moe

    ring_kinds = ("probs", "q_in", "k_in", "x_in", "v_in", "maxrows", "heads_turn", "out_turn", "out_proj",
                  "x_turn", "route", "shared_out", "positions", "order", "sorted_in", "hid_turn", "expert_out")
    ring_items = [it for it in plan if it[0] in ring_kinds and it not in (("x_in", 0), ("v_in", 0))]
    turn_of = {it: n for n, it in enumerate(ring_items)}

    def upto(kind, item):
        return [it for it in plan if it[0] == kind].index(item) + 1

    ctx = ExitStack()
    with ctx:
        def sb(name, shape, dt):
            return ctx.enter_context(nc.sbuf_tensor(name, shape, dt))

        def sem(name):
            return ctx.enter_context(nc.semaphore(name))

        ident = sb("ident", [P, P], F32)
        ident_bf = sb("ident_bf", [P, P], BF16)
        mask_qk = sb("mask_qk", [P, P], BF16)
        x_sb = sb("x_sb", [P, NT, D], F32)
        xT = sb("xT", [P, 2, BLK], F32)
        wT = sb("wT", [P, 4, D], F32)
        r_nat = sb("r_nat", [E, D], F32)
        rT = sb("rT", [P, E], F32)
        bias_qk = sb("bias_qk", [P, 2], F32)
        bias_vo = sb("bias_vo", [P, 2, D], F32)
        qk_f = sb("qk_f", [P, 2, 2, BLK], F32)
        qk_parts = sb("qk_parts", [P, 2, 2, PARTS, BLK], BF16)
        q_stack = sb("q_stack", [P, 2, H, BLK], BF16)
        k_stack = sb("k_stack", [P, NB, H, BLK], BF16)
        v_aug = sb("v_aug", [P, NT, H * VC + 32 - VC], F32)
        probs = sb("probs", [P, RING, BLK], F32)
        part_max = sb("part_max", [P, 2, TPB, 4, NB], F32)
        neg_max = sb("neg_max", [P, 2, TPB, 4], F32)
        max_parts = sb("max_parts", [P, 2, TPB, PARTS, 4], BF16)
        max_rows = sb("max_rows", [PARTS * 4, 2, BLK], BF16)
        oT = sb("oT", [P, 2, G, BLK], F32)
        w_nat = oT[:, 0, 0, :].rearrange("p (i d) -> p i d", i=4)
        denom_inv = sb("denom_inv", [P, H], F32)
        o_norm = sb("o_norm", [P, H, HD], F32)
        o_normT = sb("o_normT", [P, P], F32)
        y_res = sb("y_res", [P, D], F32)
        stats = sb("stats", [P, 6], F32)
        moments = sb("moments", [P, 2, TPB, 2], F32)
        rstd = sb("rstd", [P, 2, TPB], F32)
        minus_half = sb("minus_half", [P, TPB], F32)
        w_gu = sb("w_gu", [P, NE, 2 * FF], F32)
        wd = sb("wd", [P, NE, FC, D], F32)
        x1T = [xT[:, 0, :], xT[:, 1, :], qk_f[:, 0, 0, :], qk_f[:, 0, 1, :]]
        xs = qk_f[:, 1, 0, :].rearrange("p (t d) -> p t d", t=TPB)
        logits = sb("logits", [P, TPB, E], F32)
        top = sb("top", [P, TPB], F32)
        best = sb("best", [P, TPB], F32)
        rank = sb("rank", [P, TPB, E], F32)
        order = sb("order", [P, E], F32)
        score = sb("score", [P, TPB], F32)
        hot = sb("hot", [P, NT, E], BF16)
        hot_before = sb("hot_before", [P, NT + 1, E], BF16)
        after_q = q_stack[:, :, :, :].rearrange("p a h t -> p (a h t)").bitcast(F32)
        after_k = k_stack[:, :, :, :].rearrange("p b h t -> p (b h t)").bitcast(F32)

        def carve(region, shapes):
            at, made = 0, []
            for *shape, dt in shapes:
                n = 1
                for d in shape:
                    n *= d
                words = n // 2 if dt in (F16, BF16) else n
                view = region[:, at:at + words]
                view = view if dt == F32 else view.bitcast(dt)
                names = "abc"[:len(shape)]
                sizes = dict(zip(names, shape))
                made.append(view.rearrange(f"p ({' '.join(names)}) -> p {' '.join(names)}", **sizes))
                at += words
            assert at <= region.shape[1]
            return made

        sig, hid = carve(after_q, [(2, BLK, F32), (4, BLK, F32)])
        (xg, xgT, x_hid, x_hidT, x_out, yg, y_out, place_hot, tile_hot) = carve(after_k, [
            (NX, D, F32), (4, P, F32), (4, FF, F32), (2, FF, F32), (4, D, F32), (NT, D, F32), (NT, D, F32),
            (NT, P, F16), (NT, NX + 1, F16)])
        (column, tile_no, full_tiles, lower, token) = carve(after_q[:, 6 * BLK:], [
            (P, F32), (NX, F32), (NT, F32), (E, E, F32), (NT, F32)])
        (counts, n_tiles, start, end, base, expert_f, slot_f, place_f, tile_f, expert_i, slot_i, place_i, tile_i,
         source_i) = carve(after_q[:, 8 * BLK:], [
            (E, F32), (E, F32), (E, F32), (E, F32), (E, F32), (NX, F32), (NT, F32), (NT, F32), (NT, F32), (NX, I32),
            (NT, I32), (NT, I32), (NT, I32), (NX, I32)])
        (earlier, ones_bf) = carve(after_q[:, 12 * BLK:], [(P, BF16), (P, BF16)])
        (filled, summed, slots, before) = carve(after_q[:, 10 * BLK:], [
            (E, NT, F32), (E, E, F32), (NT, E, F32), (NX, E, F32)])

        parts_dram = nc.dram_tensor("parts_dram", (2, NB, PARTS, P, BLK), BF16, kind="Internal").ap()

        xs_dram = nc.dram_tensor("xs_dram", (T, D), F32, kind="Internal").ap()
        sorted_dram = nc.dram_tensor("sorted_dram", (NX * P, D), F32, kind="Internal").ap()

        score_ps = ctx.enter_context(nc.psum_tensor("score_ps", [P, 2, 2, BLK], F32))
        ring_ps = ctx.enter_context(nc.psum_tensor("ring_ps", [P, BANKS, BLK], F32))
        out_ps = ctx.enter_context(nc.psum_tensor("out_ps", [P, BLK], F32))

        def bank(it):
            if it == ("x_in", 0):
                return out_ps[:, :]
            if it == ("v_in", 0):
                return score_ps[:, 0, 0, :]
            return ring_ps[:, turn_of[it] % BANKS, :]

        x_loaded = [sem(f"x_loaded{b}") for b in range(NB)]
        proj_loaded = sem("proj_loaded")
        bias_loaded = sem("bias_loaded")
        moe_loaded = sem("moe_loaded")
        pool_step = sem("pool_step")
        k_filled = sem("k_filled")
        q_filled = sem("q_filled")
        consts_ready = sem("consts_ready")
        w_turned = sem("w_turned")
        w_kept = sem("w_kept")
        x_turned = sem("x_turned")
        x_kept = sem("x_kept")
        qk_made = sem("qk_made")
        q_kept = sem("q_kept")
        k_kept = sem("k_kept")
        v_made = sem("v_made")
        v_kept = sem("v_kept")
        q_split = sem("q_split")
        k_split = sem("k_split")
        bo_added = sem("bo_added")
        q_sent = [sem(f"q_sent{b}") for b in range(NB)]
        k_sent = [sem(f"k_sent{b}") for b in range(NB)]
        q_stacked = [sem(f"q_stacked{b}") for b in range(NB)]
        k_stacked = [sem(f"k_stacked{b}") for b in range(NB)]
        dve_step = sem("dve_step")
        scores_ready = sem("scores_ready")
        scores_read = sem("scores_read")
        neg_max_ready = sem("neg_max_ready")
        max_turned = sem("max_turned")
        max_rows_kept = sem("max_rows_kept")
        max_rows_placed = [sem(f"max_rows_placed{i}") for i in range(2)]
        logits_ready = sem("logits_ready")
        exp_in_ready = sem("exp_in_ready")
        probs_ready = sem("probs_ready")
        probs_masked = sem("probs_masked")
        values_done = sem("values_done")
        out_kept = sem("out_kept")
        heads_turned = sem("heads_turned")
        heads_normed = sem("heads_normed")
        out_turned = sem("out_turned")
        out_turn_kept = sem("out_turn_kept")
        out_projected = sem("out_projected")
        x1_ready = sem("x1_ready")
        y_made = sem("y_made")
        var1_ready = sem("var1_ready")
        rstd1_ready = sem("rstd1_ready")
        var2_ready = sem("var2_ready")
        rstd2_ready = sem("rstd2_ready")
        x1_turned = sem("x1_turned")
        x1T_kept = sem("x1T_kept")
        logits_read = sem("logits_read")
        top_ready = sem("top_ready")
        score_tanh = sem("score_tanh")
        xs_ready = sem("xs_ready")
        xs_stored = [sem(f"xs_stored{b}") for b in range(NB)]
        hot_ready = sem("hot_ready")
        hot_summed = sem("hot_summed")
        mix_consts = sem("mix_consts")
        shared_made = sem("shared_made")
        shared_tanh = sem("shared_tanh")
        shared_ready = sem("shared_ready")
        shared_out_made = sem("shared_out_made")
        shared_added = sem("shared_added")
        positions_made = sem("positions_made")
        positions_read = sem("positions_read")
        places_ready = sem("places_ready")
        experts_ready = sem("experts_ready")
        order_made = sem("order_made")
        order_ready = sem("order_ready")
        gathered = [sem(f"gathered{k}") for k in range(NX)]
        sorted_turned = sem("sorted_turned")
        sorted_kept = sem("sorted_kept")
        gate_up_made = sem("gate_up_made")
        gate_tanh = sem("gate_tanh")
        expert_hid_ready = sem("expert_hid_ready")
        hid_turned = sem("hid_turned")
        hid_kept = sem("hid_kept")
        expert_out_made = sem("expert_out_made")
        expert_out_kept = sem("expert_out_kept")
        expert_out_stored = [sem(f"expert_out_stored{i}") for i in range(4)]
        returned = [sem(f"returned{b}") for b in range(NB)]
        y2_made = sem("y2_made")
        y_ready = sem("y_ready")
        y_stored = sem("y_stored")

        block = ctx.enter_context(nc.Block())

        x_tiles = x.rearrange("a (n p) d -> p (a n) d", p=P)
        out_tiles = out.rearrange("a (n p) d -> p (a n) d", p=P)

        STACKED = 16
        CLEARED = 16

        units_before = {B: sum(1 for it in plan if it[0] == "probs" and it[2] < B) for B in range(NB + 1)}

        def last_quad(s):
            B, g = divmod(s, G)
            return next(it[1:] for it in plan if it[0] == "values" and it[2:] == (B, g, TPB * (B + 1) - 1))

        @block.sync
        def _(sp):
            for i, w in enumerate((Wq, Wk, Wv, Wo)):
                sp.dma_start(w_nat[:, i, :], w).then_inc(proj_loaded, 16)
            sp.dma_start(r_nat[:, :], router_w).then_inc(proj_loaded, 16)
            for b in range(1, NB):
                sp.dma_start(x_sb[:, TPB * b:TPB * b + TPB, :],
                             x_tiles[:, TPB * b:TPB * b + TPB, :]).then_inc(x_loaded[b], 16)

            def send(side, b):
                sp.wait_ge((q_split, k_split)[side], b + 1)
                sp.dma_start(parts_dram[side, b].rearrange("a p t -> p a t"),
                             qk_parts[:, side, b % 2, :, :]).then_inc((q_sent, k_sent)[side][b], 16)

            def stack_q(b):
                sp.wait_ge(q_filled, min(b, 1) + 1)
                if b >= 2:
                    sp.wait_ge(exp_in_ready, units_before[b - 1])
                    sp.dma_start(q_stack[STACK:STACK + PARTS, b % 2, :, :],
                                 q_stack[STACK + PARTS:STACK + 2 * PARTS, b % 2, :, :]).then_inc(q_stacked[b], 16)
                sp.wait_ge(q_sent[b], 16)
                rows = parts_dram[0, b].rearrange("a (o d h) t -> o (a d) (h t)", o=1, d=HD)
                sp.dma_start(q_stack[0:STACK, b % 2, :, :],
                             rows.to_broadcast([PARTS, PARTS * HD, H * BLK])).then_inc(q_stacked[b], 16)

            def stack_k(b):
                sp.wait_ge(k_filled, b + 1)
                sp.wait_ge(k_sent[b], 16)
                for r in range(PARTS):
                    rows = parts_dram[1, b, r].rearrange("(o d h) t -> o d (h t)", o=1, d=HD)
                    sp.dma_start(k_stack[r * PARTS * HD:(r + 1) * PARTS * HD, b, :, :],
                                 rows.to_broadcast([PARTS, HD, H * BLK])).then_inc(k_stacked[b], 16)

            send(0, 0)
            send(1, 0)
            stack_q(0)
            stack_k(0)
            for half, (w, s) in enumerate(((w_gate, s_gate), (w_up, s_up))):
                columns = slice(half * FF, (half + 1) * FF)
                sp.dma_start(w_gu[:, 0:E, columns], w.rearrange("e d f -> d e f")).then_inc(moe_loaded, 16)
                sp.dma_start(w_gu[:, E, columns], s).then_inc(moe_loaded, 16)
            for e in range(E):
                sp.dma_start(wd[:, e, :, :], w_down[e].rearrange("(c p) d -> p c d", p=P)).then_inc(moe_loaded, 16)
            sp.dma_start(wd[:, E, :, :], s_down.rearrange("(c p) d -> p c d", p=P)).then_inc(moe_loaded, 16)
            for it in plan:
                if it[0] == "v_in" and it[1] >= 1:
                    send(0, it[1])
                    send(1, it[1])
                    stack_q(it[1])
                    stack_k(it[1])
                elif it[0] == "maxrows":
                    s = it[1]
                    B, g = divmod(s, G)
                    sp.wait_ge(max_rows_kept, s + 1)
                    sp.dma_start(q_stack[STACK:STACK + PARTS, B % 2, 4 * g:4 * g + 4, :],
                                 max_rows[:, s % 2, :]).then_inc(max_rows_placed[s % 2], 16)
                elif it[0] == "route":
                    b = it[1]
                    sp.wait_ge(xs_ready, b + 1)
                    sp.dma_start(xs_dram[b * BLK:(b + 1) * BLK, :].rearrange("(t p) d -> p t d", p=P),
                                 xs[:, :, :]).then_inc(xs_stored[b], 16)
                elif it[0] == "expert_out":
                    k = it[1]
                    sp.wait_ge(expert_out_kept, k + 1)
                    sp.dma_start(sorted_dram[k * P:(k + 1) * P, :], x_out[:, k % 4, :]).then_inc(expert_out_stored[k % 4], 16)
                elif it[0] == "norm2":
                    b = it[1]
                    sp.wait_ge(y_ready, b + 1)
                    sp.dma_start(out_tiles[:, TPB * b:TPB * b + TPB, :],
                                 y_out[:, TPB * b:TPB * b + TPB, :]).then_inc(y_stored, 16)
            sp.wait_ge(y_stored, 16 * NB)

        @block.gpsimd
        def _(pool):
            pool.memset(ident[:, :], 0.0).then_inc(pool_step, 1)
            pool.memset(mask_qk[:, :], 0.0).then_inc(pool_step, 1)
            pool.wait_ge(pool_step, 2)
            pool.affine_select(out=ident[:, :], in_=ident[:, :], compare_op=ALU.not_equal, fill=1.0,
                               base=0, pattern=[[-1, P]], channel_multiplier=1).then_inc(pool_step, 1)
            pool.wait_ge(pool_step, 3)
            pool.tensor_copy(ident_bf[:, :], ident[:, :]).then_inc(pool_step, 1)
            pool.affine_select(out=mask_qk[:, :], in_=mask_qk[:, :], compare_op=ALU.is_ge, fill=MASKED,
                               base=0, pattern=[[-1, P]], channel_multiplier=1).then_inc(pool_step, 1)
            pool.wait_ge(pool_step, 5)
            for b in range(NB):
                ones_pair = k_stack[64:96, b, :, :].bitcast(F32)
                pool.memset(ones_pair, ONES_PAIR).then_inc(k_filled, 1)
                pool.wait_ge(k_filled, b + 1)
                if b == 0:
                    pool.memset(v_aug[:, :, :], 1.0).then_inc(consts_ready, 1)
                    pool.wait_ge(consts_ready, 1)
                    pool.memset(q_stack[64:96, 1, :, :].bitcast(F32), 0.0).then_inc(q_filled, 1)
                    pool.wait_ge(q_filled, 2)
            for e in range(E):
                pool.memset(order[:, e:e + 1], float(E - e)).then_inc(consts_ready, 1)
            pool.memset(hot_before[:, 0, :], 0.0).then_inc(consts_ready, 1)
            steps = 5
            pool.memset(minus_half[:, :], -0.5).then_inc(pool_step, 1)
            steps += 1
            pool.wait_ge(pool_step, steps)
            pool.wait_ge(bias_loaded, 64)
            for it in plan:
                kind = it[0]
                if kind == "v_in":
                    b = it[1]
                    pool.wait_ge(x_turned, b + 1)
                    here = x_sb[:, TPB * b:TPB * b + TPB, :]
                    pool.tensor_tensor(here, here, bias_vo[:, 1:2, :].to_broadcast([P, TPB, D]),
                                       ALU.add).then_inc(bo_added, 1)
                elif kind == "probs":
                    _, n, B, g, j, i = it
                    if i == 3 and j >= TPB * B:
                        pool.wait_ge(probs_ready, n + 1)
                        first = (n - 3) % RING
                        square = probs[:, first:first + 4, 0:P]
                        pool.affine_select(out=square, in_=square, compare_op=ALU.is_ge, fill=0.0, base=0,
                                           pattern=[[0, 4], [1, P]], channel_multiplier=-1).then_inc(probs_masked, 1)
                elif kind == "out_proj":
                    T0 = it[1]
                    pool.wait_ge(var1_ready, T0 + 1)
                    pool.tensor_tensor(rstd[:, 0, T0 % TPB:T0 % TPB + 1], rstd[:, 0, T0 % TPB:T0 % TPB + 1],
                                       minus_half[:, 0:1], ALU.pow).then_inc(rstd1_ready, 1)
                elif kind == "keep" and it[1] == NB * G - 1:
                    pool.wait_ge(values_done, n_quads)
                    pool.iota(column[:, :], [[1, P]], base=0, channel_multiplier=0,
                              allow_small_or_imprecise_dtypes=True).then_inc(mix_consts, 1)
                    pool.iota(tile_no[:, :], [[1, NX]], base=0, channel_multiplier=0,
                              allow_small_or_imprecise_dtypes=True).then_inc(mix_consts, 1)
                    pool.iota(full_tiles[:, :], [[P, NT]], base=0, channel_multiplier=0,
                              allow_small_or_imprecise_dtypes=True).then_inc(mix_consts, 1)
                    pool.iota(token[:, :], [[P, NT]], base=0, channel_multiplier=1,
                              allow_small_or_imprecise_dtypes=True).then_inc(mix_consts, 1)
                    pool.memset(lower[:, :, :], 1.0).then_inc(mix_consts, 1)
                    pool.memset(ones_bf[:, :], 1.0).then_inc(mix_consts, 1)
                    pool.wait_ge(mix_consts, 6)
                    pool.affine_select(out=earlier[:, :], in_=ones_bf[:, :], compare_op=ALU.is_ge, fill=0.0, base=-1,
                                       pattern=[[1, P]], channel_multiplier=-1).then_inc(mix_consts, 1)
                    pool.affine_select(out=lower[:, :, :], in_=lower[:, :, :], compare_op=ALU.is_ge, fill=0.0,
                                       base=-1, pattern=[[1, E], [-1, E]], channel_multiplier=0).then_inc(mix_consts, 1)
                elif kind == "route":
                    b = it[1]
                    pool.wait_ge(hot_ready, b + 1)
                    if b == 0:
                        pool.wait_ge(consts_ready, 2 + E)
                    for t in range(TPB * b, TPB * b + TPB):
                        pool.tensor_tensor(hot_before[:, t + 1, :], hot_before[:, t, :], hot[:, t, :],
                                           ALU.add).then_inc(hot_summed, 1)
                        pool.wait_ge(hot_summed, t + 1)
                elif kind == "order":
                    pool.wait_ge(order_ready, 1)
                    for b in range(NB):
                        pool.wait_ge(xs_stored[b], 16)
                    for k in range(NX):
                        pool.indirect_dma_start(
                            out=xg[:, k, :], out_offset=None, in_=xs_dram[:, :],
                            in_offset=bass.IndirectOffsetOnAxis(ap=source_i[:, k:k + 1], axis=0),
                            bounds_check=T - 1).then_inc(gathered[k], 16)
                elif kind == "moments2":
                    b = it[1]
                    if b == 0:
                        for i in range(4):
                            pool.wait_ge(expert_out_stored[i], 16 * len(range(i, NX, 4)))
                        for c in range(NB):
                            for t in range(TPB * c, TPB * c + TPB):
                                pool.indirect_dma_start(
                                    out=yg[:, t, :], out_offset=None, in_=sorted_dram[:, :],
                                    in_offset=bass.IndirectOffsetOnAxis(ap=slot_i[:, t:t + 1], axis=0),
                                    bounds_check=NX * P - 1).then_inc(returned[c], 16)
                            if c:
                                pool.wait_ge(var2_ready, c)
                                pool.tensor_tensor(rstd[:, 1, :], rstd[:, 1, :], minus_half[:, :],
                                                   ALU.pow).then_inc(rstd2_ready, 1)
                        pool.wait_ge(var2_ready, NB)
                        pool.tensor_tensor(rstd[:, 1, :], rstd[:, 1, :], minus_half[:, :],
                                           ALU.pow).then_inc(rstd2_ready, 1)

        @block.scalar
        def _(act):
            act.dma_start(x_sb[:, 0:TPB, :], x_tiles[:, 0:TPB, :]).then_inc(x_loaded[0], 16)
            for i, bias in enumerate((bq, bk)):
                act.dma_start(bias_qk[:, i:i + 1], bias.rearrange("(h d) -> d h", d=HD),
                              allow_slow_non_contiguous=True).then_inc(bias_loaded, 16)
            for i, bias in enumerate((bv, bo)):
                act.dma_start(bias_vo[:, i, :], bias.rearrange("(a d) -> a d", a=1).to_broadcast([P, D])
                              ).then_inc(bias_loaded, 16)
            act.wait_ge(w_turned, 1)
            for i in range(2):
                act.activation(wT[:, i, :].rearrange("p (d h) -> p d h", d=HD),
                               score_ps[:, 1, 0, i * D:(i + 1) * D].rearrange("p (h d) -> p d h", d=HD), ACT.Copy).then_inc(w_kept, 1)
            act.activation(wT[:, 2:4, :], score_ps[:, 1, 0, 2 * D:4 * D].rearrange("p (i d) -> p i d", i=2), ACT.Copy).then_inc(w_kept, 1)
            act.wait_ge(w_turned, 2)
            act.activation(rT[:, :], score_ps[:, 1, 1, 0:E], ACT.Copy).then_inc(w_kept, 1)
            act.wait_ge(bias_loaded, 64)
            for it in plan:
                kind = it[0]
                if kind == "x_in":
                    b = it[1]
                    act.wait_ge(x_turned, b + 1)
                    act.activation(xT[:, b % 2, :], bank(it), ACT.Copy).then_inc(x_kept, 1)
                elif kind in ("q_in", "k_in"):
                    b = it[1]
                    side = int(kind == "k_in")
                    act.wait_ge(qk_made, 2 * b + side + 1)
                    act.activation(qk_f[:, side, b % 2, :], bank(it), ACT.Identity,
                                   bias=bias_qk[:, side:side + 1]).then_inc((q_kept, k_kept)[side], 1)
                elif kind == "probs":
                    _, n, B, g, j, i = it
                    w = BLK - P * max(0, j - TPB * B)
                    act.wait_ge(exp_in_ready, n + 1)
                    if n >= RING:
                        act.wait_ge(values_done, (n - RING) // 4 + 1)
                    act.activation(probs[:, n % RING, 0:w], bank(it)[:, 0:w], ACT.Exp,
                                   scale=SCALE).then_inc(probs_ready, 1)
                elif kind == "maxrows":
                    s = it[1]
                    act.wait_ge(max_turned, s + 1)
                    if s >= 2:
                        act.wait_ge(max_rows_placed[s % 2], 16 * (s // 2))
                    act.activation(max_rows[:, s % 2, :], bank(it)[0:4 * PARTS, :], ACT.Copy).then_inc(max_rows_kept, 1)
                elif kind == "keep":
                    s = it[1]
                    B, g = divmod(s, G)
                    act.wait_ge(values_done, upto("values", ("values", *last_quad(s))))
                    if B >= 2:
                        act.wait_ge(heads_turned, TPB * (B - 1))
                    act.activation(oT[:, B % 2, g, :], out_ps[:, :], ACT.Copy).then_inc(out_kept, 1)
                elif kind == "out_turn":
                    act.wait_ge(out_turned, it[1] + 1)
                    if it[1] >= 1:
                        act.wait_ge(out_projected, it[1])
                    act.activation(o_normT[:, :], bank(it)[:, 0:P], ACT.Copy).then_inc(out_turn_kept, 1)
                elif kind == "x_turn":
                    b = it[1]
                    act.wait_ge(x1_turned, b + 1)
                    act.activation(x1T[b], bank(it), ACT.Copy).then_inc(x1T_kept, 1)
                elif kind == "route":
                    b = it[1]
                    act.wait_ge(top_ready, b + 1)
                    act.activation(score[:, :], top[:, :], ACT.Tanh, scale=0.5).then_inc(score_tanh, 1)
                elif kind == "shared":
                    _, b, f = it
                    r = b * FC + f
                    act.wait_ge(shared_made, r + 1)
                    if r >= 2:
                        act.wait_ge(shared_ready, r - 1)
                    act.activation(sig[:, r % 2, :], score_ps[:, r % 2, 0, :], ACT.Tanh,
                                   scale=0.5).then_inc(shared_tanh, 1)
                elif kind == "sorted_in":
                    k = it[1]
                    act.wait_ge(sorted_turned, k + 1)
                    if k >= 4:
                        act.wait_ge(gate_up_made, k - 3)
                    act.activation(xgT[:, k % 4, :], bank(it)[:, 0:P], ACT.Copy).then_inc(sorted_kept, 1)
                elif kind == "gate_up":
                    k = it[1]
                    act.wait_ge(gate_up_made, k + 1)
                    if k >= 4:
                        act.wait_ge(hid_turned, k - 3)
                    act.activation(x_hid[:, k % 4, :], score_ps[:, k % 4 // 2, k % 2, 0:FF], ACT.Tanh,
                                   scale=0.5).then_inc(gate_tanh, 1)
                elif kind == "hid_turn":
                    k = it[1]
                    act.wait_ge(hid_turned, k + 1)
                    if k >= 2:
                        act.wait_ge(expert_out_made, k - 1)
                    act.activation(x_hidT[:, k % 2, :], bank(it)[:, 0:FF], ACT.Copy).then_inc(hid_kept, 1)
                elif kind == "expert_out":
                    k = it[1]
                    act.wait_ge(expert_out_made, k + 1)
                    if k >= 4:
                        act.wait_ge(expert_out_stored[k % 4], 16 * (k // 4))
                    act.activation(x_out[:, k % 4, :], bank(it)[:, 0:D], ACT.Copy, scale=0.5).then_inc(expert_out_kept, 1)

        @block.vector
        def _(dve):
            chain = [0]

            def link(ins):
                chain[0] += 1
                ins.then_inc(dve_step, 1)
                dve.wait_ge(dve_step, chain[0])

            def moments_of(which, t, src):
                link(dve.bn_stats(stats[:, :], src))
                link(dve.bn_aggr(moments[:, which, t, :], stats[:, :]))
                return dve.tensor_scalar(rstd[:, which, t:t + 1], moments[:, which, t, 1:2], LN_EPS, None, ALU.add)

            def normalised(which, t, dst, src):
                return dve.tensor_scalar(dst, src, moments[:, which, t, 0:1], rstd[:, which, t:t + 1],
                                         ALU.subtract, ALU.mult)

            dve.memset(q_stack[64:96, 0, :, :].bitcast(F32), 0.0).then_inc(q_filled, 1)
            dve.wait_ge(bias_loaded, 64)

            for it in plan:
                kind = it[0]
                if kind in ("q_in", "k_in"):
                    b = it[1]
                    side = int(kind == "k_in")
                    dve.wait_ge((q_kept, k_kept)[side], b + 1)
                    if b >= 2:
                        dve.wait_ge((q_sent, k_sent)[side][b - 2], 16)
                    rest = qk_f[:, side, b % 2, :]
                    for a in range(PARTS):
                        part = qk_parts[:, side, b % 2, a, :]
                        copied = dve.tensor_copy(part, rest)
                        if a == PARTS - 1:
                            copied.then_inc((q_split, k_split)[side], 1)
                            break
                        link(copied)
                        link(dve.tensor_tensor(rest, rest, part, ALU.subtract))
                elif kind == "v_in":
                    b = it[1]
                    dve.wait_ge(v_made, b + 1)
                    dve.wait_ge(consts_ready, 1)
                    for t in range(TPB):
                        dst = v_aug[:, TPB * b + t, 0:H * VC].rearrange("p (h c) -> p h c", c=VC)[:, :, 0:HD]
                        last = dve.tensor_tensor(
                            dst, bank(it)[:, t * P:(t + 1) * P].rearrange("p (h c) -> p h c", c=HD),
                            bias_vo[:, 0, :].rearrange("p (h c) -> p h c", c=HD), ALU.add)
                    last.then_inc(v_kept, 1)
                elif kind == "scores":
                    _, m, B, g, t, c, hp = it
                    w = min(BLK, P * (TPB * B + t + 1) - BLK * c)
                    s = G * B + g
                    dve.wait_ge(scores_ready, m + 1)
                    dve.tensor_reduce(out=part_max[:, s % 2, t, 2 * hp:2 * hp + 2, c], in_=score_ps[:, m % 2, :, 0:w],
                                      axis=AX.X, op=ALU.max).then_inc(scores_read, 1)
                elif kind == "negmax":
                    s = it[1]
                    B = s // G
                    dve.wait_ge(scores_read, sum(2 * TPB * (q // G + 1) for q in range(s + 1)))
                    if s >= 2:
                        dve.wait_ge(max_turned, s - 1)
                    rest = neg_max[:, s % 2, :, :]
                    link(dve.tensor_reduce(out=rest, in_=part_max[:, s % 2, :, :, 0:B + 1],
                                           axis=AX.X, op=ALU.max, negate=True))
                    for a in range(PARTS):
                        part = max_parts[:, s % 2, :, a, :]
                        copied = dve.tensor_copy(part, rest)
                        if a == PARTS - 1:
                            copied.then_inc(neg_max_ready, 1)
                            break
                        link(copied)
                        link(dve.tensor_tensor(rest, rest, part, ALU.subtract))
                elif kind == "heads_turn":
                    T0 = it[1]
                    dve.wait_ge(heads_turned, T0 + 1)
                    by_head = bank(it).rearrange("p (h c) -> p h c", c=32)
                    link(dve.reciprocal(denom_inv[:, :], by_head[:, :, HD]))
                    if T0 >= 1:
                        dve.wait_ge(out_turned, T0)
                    dve.tensor_tensor(o_norm[:, :, :], by_head[:, :, 0:HD],
                                      denom_inv[:, :].rearrange("p (h c) -> p h c", c=1).to_broadcast([P, H, HD]),
                                      ALU.mult).then_inc(heads_normed, 1)
                elif kind == "out_proj":
                    T0 = it[1]
                    dve.wait_ge(out_projected, T0 + 1)
                    dve.wait_ge(bo_added, T0 // TPB + 1)
                    dve.tensor_tensor(y_res[:, :], bank(it)[:, 0:D], x_sb[:, T0, :], ALU.add).then_inc(y_made, 1)
                    dve.wait_ge(y_made, T0 + 1)
                    moments_of(0, T0 % TPB, y_res[:, :]).then_inc(var1_ready, 1)
                elif kind == "norm1":
                    T0 = it[1]
                    dve.wait_ge(rstd1_ready, T0 + 1)
                    normalised(0, T0 % TPB, x_sb[:, T0, :], y_res[:, :]).then_inc(x1_ready, 1)
                    dve.wait_ge(x1_ready, T0 + 1)
                elif kind == "route":
                    b = it[1]
                    dve.wait_ge(logits_ready, b + 1)
                    dve.tensor_copy(logits[:, :, :], bank(it)[:, 0:TPB * E].rearrange("p (t e) -> p t e", e=E)).then_inc(logits_read, 1)
                    dve.wait_ge(logits_read, b + 1)
                    if b >= 1:
                        dve.wait_ge(xs_ready, b)
                    dve.tensor_reduce(out=top[:, :], in_=logits[:, :, :], axis=AX.X, op=ALU.max).then_inc(top_ready, 1)
                    dve.wait_ge(top_ready, b + 1)
                    spread = lambda v: v.rearrange("p (t a) -> p t a", a=1).to_broadcast([P, TPB, E])
                    link(dve.tensor_tensor(rank[:, :, :], logits[:, :, :], spread(top[:, :]), ALU.is_equal))
                    if b == 0:
                        dve.wait_ge(consts_ready, 1 + E)
                    link(dve.tensor_tensor(rank[:, :, :], rank[:, :, :],
                                           order[:, :].rearrange("p (a e) -> p a e", a=1).to_broadcast([P, TPB, E]), ALU.mult))
                    link(dve.tensor_reduce(out=best[:, :], in_=rank[:, :, :], axis=AX.X, op=ALU.max))
                    dve.tensor_tensor(hot[:, TPB * b:TPB * b + TPB, :], rank[:, :, :], spread(best[:, :]),
                                      ALU.is_equal).then_inc(hot_ready, 1)
                    dve.wait_ge(score_tanh, b + 1)
                    if b >= 1:
                        dve.wait_ge(xs_stored[b - 1], 16)
                    link(dve.tensor_scalar(score[:, :], score[:, :], 0.5, 0.5, ALU.mult, ALU.add))
                    for t in range(TPB):
                        last = dve.tensor_scalar(xs[:, t, :], x_sb[:, TPB * b + t, :], score[:, t:t + 1], None, ALU.mult)
                    last.then_inc(xs_ready, 1)
                elif kind == "shared":
                    _, b, f = it
                    r = b * FC + f
                    dve.wait_ge(shared_tanh, r + 1)
                    link(dve.scalar_tensor_tensor(out=sig[:, r % 2, :], in0=sig[:, r % 2, :], scalar=1.0,
                                                  in1=score_ps[:, r % 2, 0, :], op0=ALU.add, op1=ALU.mult))
                    if r >= 4:
                        dve.wait_ge(shared_out_made, r // FC - 1)
                    dve.tensor_tensor(hid[:, r % 4, :], sig[:, r % 2, :], score_ps[:, r % 2, 1, :],
                                      ALU.mult).then_inc(shared_ready, 1)
                elif kind == "shared_out":
                    b = it[1]
                    dve.wait_ge(shared_out_made, b + 1)
                    so_far = x_sb[:, TPB * b:TPB * b + TPB, :].rearrange("p t d -> p (t d)")
                    dve.scalar_tensor_tensor(out=so_far, in0=bank(it), scalar=0.5, in1=so_far,
                                             op0=ALU.mult, op1=ALU.add).then_inc(shared_added, 1)
                elif kind == "positions":
                    dve.wait_ge(positions_made, 1)
                    dve.wait_ge(mix_consts, 8)

                    def over(v, n, inner):
                        m = v.shape[1]
                        if inner:
                            return v.rearrange("p (m a) -> p m a", a=1).to_broadcast([P, m, n])
                        return v.rearrange("p (a m) -> p a m", a=1).to_broadcast([P, n, m])

                    pos = bank(it)[:, 0:NT * E].rearrange("p (t e) -> p t e", e=E)
                    link(dve.tensor_copy(counts, bank(it)[:, NT * E:NT * E + E]))
                    link(dve.tensor_tensor(filled, over(counts, NT, True), over(full_tiles, E, False), ALU.is_gt))
                    link(dve.tensor_reduce(out=n_tiles, in_=filled, axis=AX.X, op=ALU.add))
                    link(dve.tensor_tensor(summed, lower, over(n_tiles, E, False), ALU.mult))
                    link(dve.tensor_reduce(out=start, in_=summed, axis=AX.X, op=ALU.add))
                    link(dve.tensor_scalar(base, start, float(P), None, ALU.mult))
                    dve.tensor_tensor(slots, pos, over(base, NT, False), ALU.add).then_inc(positions_read, 1)
                    dve.wait_ge(positions_read, 1)
                    link(dve.tensor_tensor(slots, slots, hot[:, :, :], ALU.mult))
                    link(dve.tensor_reduce(out=slot_f, in_=slots, axis=AX.X, op=ALU.add))
                    link(dve.tensor_copy(slot_i, slot_f))
                    link(dve.tensor_scalar(place_i, slot_i, P - 1, None, ALU.bitwise_and))
                    link(dve.tensor_scalar(tile_i, slot_i, P.bit_length() - 1, None, ALU.logical_shift_right))
                    link(dve.tensor_copy(place_f, place_i))
                    link(dve.tensor_copy(tile_f, tile_i))
                    link(dve.tensor_tensor(tile_hot[:, :, 0:NX], over(tile_f, NX, True), over(tile_no, NT, False), ALU.is_equal))
                    link(dve.tensor_tensor(tile_hot[:, :, 0:NX], tile_hot[:, :, 0:NX], over(token, NX, True), ALU.mult))
                    dve.tensor_tensor(place_hot, over(place_f, P, True), over(column, NT, False),
                                      ALU.is_equal).then_inc(places_ready, 1)
                    link(dve.tensor_tensor(end, start, n_tiles, ALU.add))
                    link(dve.tensor_tensor(before, over(tile_no, E, True), over(end, NX, False), ALU.is_ge))
                    link(dve.tensor_reduce(out=expert_f, in_=before, axis=AX.X, op=ALU.add))
                    dve.tensor_scalar(expert_i, expert_f, float(E - 1), None, ALU.min).then_inc(experts_ready, 1)
                elif kind == "order":
                    dve.wait_ge(order_made, 1)
                    dve.tensor_copy(source_i, bank(it)[:, 0:NX]).then_inc(order_ready, 1)
                elif kind == "gate_up":
                    k = it[1]
                    dve.wait_ge(gate_tanh, k + 1)
                    both = score_ps[:, k % 4 // 2, k % 2, :]
                    link(dve.scalar_tensor_tensor(out=x_hid[:, k % 4, :], in0=x_hid[:, k % 4, :], scalar=1.0,
                                                  in1=both[:, 0:FF], op0=ALU.add, op1=ALU.mult))
                    dve.tensor_tensor(x_hid[:, k % 4, :], x_hid[:, k % 4, :], both[:, FF:2 * FF],
                                      ALU.mult).then_inc(expert_hid_ready, 1)
                elif kind == "moments2":
                    b = it[1]
                    dve.wait_ge(returned[b], 16 * TPB)
                    dve.wait_ge(shared_added, b + 1)
                    here = x_sb[:, TPB * b:TPB * b + TPB, :]
                    dve.tensor_tensor(here, here, yg[:, TPB * b:TPB * b + TPB, :], ALU.add).then_inc(y2_made, 1)
                    dve.wait_ge(y2_made, b + 1)
                    for t in range(TPB):
                        made = moments_of(1, t, x_sb[:, TPB * b + t, :])
                        if t < TPB - 1:
                            link(made)
                    made.then_inc(var2_ready, 1)
                elif kind == "norm2":
                    b = it[1]
                    dve.wait_ge(rstd2_ready, b + 1)
                    for t in range(TPB * b, TPB * b + TPB):
                        last = normalised(1, t % TPB, y_out[:, t, :], x_sb[:, t, :])
                    last.then_inc(y_ready, 1)

        @block.tensor
        def _(pe):
            mm, turn = pe.matmul, pe.transpose

            pe.wait_ge(pool_step, 5)
            pe.wait_ge(proj_loaded, 16 * 5)
            for i in range(4):
                last = turn(score_ps[:, 1, 0, i * P:(i + 1) * P], w_nat[:, i, :], ident[:, :])
            last.then_inc(w_turned, 1)
            turn(score_ps[:, 1, 1, 0:E], r_nat[:, :], ident[0:E, 0:E]).then_inc(w_turned, 1)
            def wait_bank(it):
                u = turn_of[it] - BANKS
                if u < 0:
                    return
                last = ring_items[u]
                read = {"probs": probs_ready, "x_in": x_kept, "q_in": q_kept, "k_in": k_kept, "v_in": v_kept,
                        "maxrows": max_rows_kept, "heads_turn": heads_normed, "out_turn": out_turn_kept,
                        "out_proj": y_made, "x_turn": x1T_kept, "route": logits_read,
                        "shared_out": shared_added, "positions": positions_read, "order": order_ready,
                        "sorted_in": sorted_kept, "hid_turn": hid_kept, "expert_out": expert_out_kept}[last[0]]
                pe.wait_ge(read, (last[1] if len(last) > 1 else 0) + 1)

            for it in plan:
                kind = it[0]
                if kind == "x_in":
                    b = it[1]
                    if b >= 1:
                        wait_bank(it)
                    pe.wait_ge(x_loaded[b], 16)
                    for t in range(TPB):
                        last = turn(bank(it)[:, t * P:(t + 1) * P], x_sb[:, TPB * b + t, :], ident[:, :])
                    last.then_inc(x_turned, 1)
                elif kind in ("q_in", "k_in"):
                    b = it[1]
                    side = int(kind == "k_in")
                    wait_bank(it)
                    if b == 0:
                        pe.wait_ge(w_kept, 3)
                    pe.wait_ge(x_kept, b + 1)
                    mm(bank(it), wT[:, side, :], xT[:, b % 2, :], start=True, stop=True).then_inc(qk_made, 1)
                elif kind == "v_in":
                    b = it[1]
                    if b >= 1:
                        wait_bank(it)
                    for t in range(TPB):
                        last = mm(bank(it)[:, t * P:(t + 1) * P], xT[:, b % 2, t * P:(t + 1) * P], wT[:, 2, :],
                                  start=True, stop=True)
                    last.then_inc(v_made, 1)
                elif kind == "scores":
                    _, m, B, g, t, c, hp = it
                    T0 = TPB * B + t
                    w = min(BLK, P * (T0 + 1) - BLK * c)
                    if m >= 2:
                        pe.wait_ge(scores_read, m - 1)
                    elif m == 0:
                        pe.wait_ge(v_kept, 1)
                    elif m == 1:
                        pe.wait_ge(w_kept, 4)
                    if g == 0 and t == 0:
                        pe.wait_ge(k_stacked[c], STACKED * PARTS)
                        pe.wait_ge(q_stacked[B], STACKED + (CLEARED if B >= 2 else 0))
                    for i in range(2):
                        h = 4 * g + 2 * hp + i
                        last = mm(score_ps[:, m % 2, i, 0:w], q_stack[0:KROWS, B % 2, h, t * P:(t + 1) * P],
                                  k_stack[0:KROWS, c, h, 0:w], start=True, stop=c < B)
                        if c == B:
                            last = mm(score_ps[:, m % 2, i, w - P:w], ident_bf[:, :], mask_qk[:, :],
                                      start=False, stop=True)
                    last.then_inc(scores_ready, 1)
                elif kind == "maxrows":
                    s = it[1]
                    wait_bank(it)
                    pe.wait_ge(neg_max_ready, s + 1)
                    for t in range(TPB):
                        last = mm(bank(it)[0:4 * PARTS, t * P:(t + 1) * P],
                                  max_parts[:, s % 2, t, :, :].rearrange("p a h -> p (a h)"), ident_bf[:, :],
                                  start=True, stop=True)
                    last.then_inc(max_turned, 1)
                elif kind == "probs":
                    _, n, B, g, j, i = it
                    s = G * B + g
                    skip = P * max(0, j - TPB * B)
                    w = BLK - skip
                    h = 4 * g + i
                    wait_bank(it)
                    if j == 0 and i == 0:
                        pe.wait_ge(max_rows_placed[s % 2], 16 * (s // 2 + 1))
                    mm(bank(it)[:, 0:w], k_stack[0:KROWS, j // TPB, h, j % TPB * P:(j % TPB + 1) * P],
                       q_stack[0:KROWS, B % 2, h, skip:BLK], start=True, stop=True).then_inc(exp_in_ready, 1)
                elif kind == "values":
                    _, k, B, g, j = it
                    s = G * B + g
                    skip = P * max(0, j - TPB * B)
                    w = BLK - skip
                    if j >= TPB * B:
                        pe.wait_ge(probs_masked, TPB * s + j - TPB * B + 1)
                    else:
                        pe.wait_ge(probs_ready, 4 * k + 4)
                    if k == 0:
                        pe.wait_ge(x_kept, 1)
                    if j == 0 and s >= 1:
                        pe.wait_ge(out_kept, s)
                    for i in range(4):
                        h = 4 * g + i
                        last = mm(out_ps[32 * i:32 * i + 32, skip:BLK], v_aug[:, j, h * VC:h * VC + 32],
                                  probs[:, (4 * k + i) % RING, 0:w], start=j == 0, stop=j == TPB * (B + 1) - 1)
                    last.then_inc(values_done, 1)
                elif kind == "heads_turn":
                    T0 = it[1]
                    B, t = divmod(T0, TPB)
                    wait_bank(it)
                    pe.wait_ge(out_kept, G * (B + 1))
                    for g in range(G):
                        last = turn(bank(it)[:, g * P:(g + 1) * P], oT[:, B % 2, g, t * P:(t + 1) * P], ident[:, :])
                    last.then_inc(heads_turned, 1)
                elif kind == "out_turn":
                    wait_bank(it)
                    pe.wait_ge(heads_normed, it[1] + 1)
                    turn(bank(it)[:, 0:P], o_norm[:, :, :].rearrange("p h c -> p (h c)"), ident[:, :]).then_inc(out_turned, 1)
                elif kind == "out_proj":
                    wait_bank(it)
                    pe.wait_ge(out_turn_kept, it[1] + 1)
                    mm(bank(it)[:, 0:D], o_normT[:, :], wT[:, 3, :], start=True, stop=True).then_inc(out_projected, 1)
                elif kind == "x_turn":
                    b = it[1]
                    wait_bank(it)
                    pe.wait_ge(x1_ready, TPB * (b + 1))
                    for t in range(TPB):
                        last = turn(bank(it)[:, t * P:(t + 1) * P], x_sb[:, TPB * b + t, :], ident[:, :])
                    last.then_inc(x1_turned, 1)
                elif kind == "route":
                    b = it[1]
                    wait_bank(it)
                    pe.wait_ge(x1T_kept, b + 1)
                    for t in range(TPB):
                        last = mm(bank(it)[:, t * E:(t + 1) * E], x1T[b][:, t * P:(t + 1) * P], rT[:, :],
                                  start=True, stop=True)
                    last.then_inc(logits_ready, 1)
                elif kind == "shared":
                    _, b, f = it
                    r = b * FC + f
                    if r == 0:
                        pe.wait_ge(moe_loaded, 16 * (4 + NE))
                        pe.wait_ge(scores_read, n_jobs)
                    if r >= 2:
                        pe.wait_ge(shared_ready, r - 1)
                    pe.wait_ge(x1T_kept, b + 1)
                    for half in range(2):
                        at = half * FF + f * P
                        last = mm(score_ps[:, r % 2, half, :], w_gu[:, E, at:at + P], x1T[b], start=True, stop=True)
                    last.then_inc(shared_made, 1)
                elif kind == "shared_out":
                    b = it[1]
                    wait_bank(it)
                    pe.wait_ge(shared_ready, FC * (b + 1))
                    for t in range(TPB):
                        for f in range(FC):
                            last = mm(bank(it)[:, t * P:(t + 1) * P], hid[:, (FC * b + f) % 4, t * P:(t + 1) * P],
                                      wd[:, E, f, :], start=f == 0, stop=f == FC - 1)
                    last.then_inc(shared_out_made, 1)
                elif kind == "positions":
                    wait_bank(it)
                    pe.wait_ge(hot_summed, NT)
                    pe.wait_ge(mix_consts, 8)
                    mm(bank(it)[:, 0:NT * E], earlier[:, :], hot[:, :, :].rearrange("p t e -> p (t e)"), start=True, stop=False)
                    mm(bank(it)[:, 0:NT * E], ones_bf[:, :], hot_before[:, 0:NT, :].rearrange("p t e -> p (t e)"),
                       start=False, stop=True)
                    mm(bank(it)[:, NT * E:NT * E + E], ones_bf[:, :], hot_before[:, NT, :],
                       start=True, stop=True).then_inc(positions_made, 1)
                elif kind == "order":
                    wait_bank(it)
                    pe.wait_ge(places_ready, 1)
                    for t in range(NT):
                        last = mm(bank(it)[:, 0:NX], place_hot[:, t, :], tile_hot[:, t, 0:NX], start=t == 0, stop=t == NT - 1)
                    last.then_inc(order_made, 1)
                elif kind == "sorted_in":
                    k = it[1]
                    wait_bank(it)
                    pe.wait_ge(gathered[k], 16)
                    turn(bank(it)[:, 0:P], xg[:, k, :], ident[:, :]).then_inc(sorted_turned, 1)
                elif kind == "gate_up":
                    k = it[1]
                    if k == 0:
                        pe.wait_ge(experts_ready, 1)
                        pe.wait_ge(shared_ready, NB * FC)
                    if k >= 4:
                        pe.wait_ge(expert_hid_ready, k - 3)
                    pe.wait_ge(sorted_kept, k + 1)
                    e = pe.value_load(expert_i[0:1, k:k + 1], min_val=0, max_val=E - 1)
                    mm(score_ps[:, k % 4 // 2, k % 2, :], xgT[:, k % 4, :], w_gu[:, bass.ds(e, 1), :].rearrange("p a n -> p (a n)"),
                       start=True, stop=True).then_inc(gate_up_made, 1)
                elif kind == "hid_turn":
                    k = it[1]
                    wait_bank(it)
                    pe.wait_ge(expert_hid_ready, k + 1)
                    for f in range(FC):
                        last = turn(bank(it)[:, f * P:(f + 1) * P], x_hid[:, k % 4, f * P:(f + 1) * P], ident[:, :])
                    last.then_inc(hid_turned, 1)
                elif kind == "expert_out":
                    k = it[1]
                    wait_bank(it)
                    pe.wait_ge(hid_kept, k + 1)
                    e = pe.value_load(expert_i[0:1, k:k + 1], min_val=0, max_val=E - 1)
                    for f in range(FC):
                        last = mm(bank(it)[:, 0:D], x_hidT[:, k % 2, f * P:(f + 1) * P],
                                  wd[:, bass.ds(e, 1), f, :].rearrange("p a n -> p (a n)"), start=f == 0, stop=f == FC - 1)
                    last.then_inc(expert_out_made, 1)


_INS = ['L0_attn_x', 'L0_attn_Wq', 'L0_attn_bq', 'L0_attn_Wk', 'L0_attn_bk', 'L0_attn_Wv', 'L0_attn_bv',
        'L0_attn_Wo', 'L0_attn_bo', 'L0_ffn_router_w', 'L0_ffn_expert_gate', 'L0_ffn_expert_up',
        'L0_ffn_expert_down', 'L0_ffn_shared_gate', 'L0_ffn_shared_up', 'L0_ffn_shared_down']
_OUTS = [((1, 2048, 128), 'float32')]


def kernel(**inputs):
    import numpy as _np
    import concourse.bacc as _bacc
    from concourse import mybir as _mybir
    from concourse.bass_utils import run_bass_kernel_spmd as _run

    nc = _bacc.Bacc("TRN2", target_bir_lowering=False, num_devices=1)
    arrays, args = {}, []
    for name in _INS:
        a = _np.ascontiguousarray(inputs[name])
        arrays[f"in_{name}_dram"] = a
        args.append(nc.dram_tensor(f"in_{name}_dram", a.shape, _mybir.dt.from_np(a.dtype), kind="ExternalInput").ap())
    for i, (shape, dtype) in enumerate(_OUTS):
        dt = _mybir.dt.from_np(_np.dtype(dtype))
        args.append(nc.dram_tensor(f"out_{i}_dram", shape, dt, kind="ExternalOutput").ap())
    block_kernel(nc, *args)
    r = _run(nc, [arrays], core_ids=[0])
    got = tuple(r.results[0][f"out_{i}_dram"] for i in range(len(_OUTS)))
    return got[0]
```

```python
import struct
from contextlib import ExitStack

import concourse.bass as bass
from concourse import mybir

F32 = mybir.dt.float32
BF16 = mybir.dt.bfloat16
F16 = mybir.dt.float16
I32 = mybir.dt.int32
ALU = mybir.AluOpType
ACT = mybir.ActivationFunctionType
AX = mybir.AxisListType

P = 128
BLK = 512
TPB = BLK // P
MASKED = -1.0e30
MINUS_ONES = struct.unpack('<f', bytes.fromhex('80bf80bf'))[0]
LN_EPS = 1e-5
PARTS = 3
LEAD = (12000, 11000, 8000, 8000)
PATIENCE = 0
HOLD = 15
EAGER = 6
LATENCY = 350
SPLIT_MAXIMA = 1600
PLACE_MAXIMA = 3000
JOB_COLUMNS = 60
LAST_RATE = 1.3
PREPARE = ("x_in", "q_in", "k_in", "v_in")
START = (0, 2, 0, 6)
BACKGROUND_UNIT = 3
SPREAD = (1, 1, 1, 2)
VALUE_LAG = 3
RING = 8
ROUTE_AT = 41
ORDER_AFTER = 4
EXPERTS_AT = 52
EARLY = 12
AHEAD = 4
GATHER_AHEAD = 4
FILL = (1, 3, 5, 3, 1)
SHARED_OUT_AT = 11
RETURN_AT = 11
MOMENTS_AT = 9


def make_plan(NB, G):
    jobs = [(B, g, t, c, hp) for B in range(NB) for g in range(G) for t in range(TPB)
            for c in range(B + 1) for hp in range(2)]
    per_step = [2 * TPB * (B + 1) for B in range(NB) for g in range(G)]
    width = lambda B, t, c: min(BLK, P * (TPB * B + t + 1) - BLK * c)
    done = [0]
    for B, g, t, c, hp in jobs:
        done.append(done[-1] + width(B, t, c) + JOB_COLUMNS)
    step_end, at = {}, 0
    for s, n in enumerate(per_step):
        at += n
        step_end[at] = s

    main, finish = [], []
    unit = quad = before = 0
    value = None
    for B in range(NB):
        background = [(k, B + 1) for k in PREPARE if 2 <= B + 1 < NB] + finish
        quads = [(g, j) for g in range(G) for j in range(TPB * (B + 1))]
        begin = done[before + per_step[G * B]]
        end = done[before + G * per_step[G * B] + per_step[G * (B + 1)]] if B < NB - 1 else begin + (done[-1] - begin) * LAST_RATE
        for ql, (g, j) in enumerate(quads):
            for i in range(4):
                due = sum(d <= begin + LEAD[B] + (ql + i / 4) / len(quads) * (end - begin) for d in done[1:])
                main.append((("probs", unit, B, g, j, i), due))
                unit += 1
                if i == BACKGROUND_UNIT and ql > START[B] and (ql - START[B]) % SPREAD[B] == 0 and background:
                    main.append((background.pop(0), due))
                if i == VALUE_LAG and value is not None:
                    main.append((value, due))
                    if value[4] == TPB * (value[2] + 1) - 1:
                        main.append((("keep", G * value[2] + value[3]), due))
            value = ("values", quad, B, g, j)
            quad += 1
        before += len(quads) * 2
        assert not background
        finish = [(k, TPB * B + t) for t in range(TPB) for k in ("heads_turn", "out_turn", "out_proj", "norm1")]

    costs = {"x_in": (436, "scalar", 478, 0), "q_in": (858, "vector", 602, 1400), "k_in": (858, "vector", 602, 1400),
             "v_in": (872, "vector", 810, 0), "maxrows": (212, "scalar", 478, 0), "heads_turn": (436, "vector", 410, 0),
             "out_turn": (109, "scalar", 158, 0), "out_proj": (218, "vector", 200, 800)}
    clock = {"tensor": 0.0, "vector": 0.0, "scalar": 0.0}
    slots, ring, exp_done, max_ready, max_placed = [0.0, 0.0], [0.0] * 3, {}, {}, {}
    plan, job, turns = [], 0, 0

    def start_of(item):
        if item[0] == "scores":
            return max(clock["tensor"], slots[item[1] % 2])
        if item[0] == "values":
            return max(clock["tensor"], exp_done[item[2:]])
        if item[0] == "maxrows":
            return max(clock["tensor"], max_ready[item[1]], ring[turns % 3])
        if item[0] == "probs":
            s = G * item[2] + item[3]
            in_place = max_placed[s] if s in max_placed else max(max_ready[s], clock["tensor"]) + PLACE_MAXIMA
            return max(clock["tensor"], ring[turns % 3], in_place)
        if item[0] in costs:
            return max(clock["tensor"], ring[turns % 3])
        return clock["tensor"]

    def put(item):
        nonlocal job, turns
        kind = item[0]
        clock["tensor"] = start_of(item)
        plan.append(item)
        if kind == "scores":
            _, m, B, g, t, c, hp = item
            w = width(B, t, c)
            clock["tensor"] += 0.84 * w + 8 + 107 * (c == B)
            slots[m % 2] = clock["vector"] = max(clock["vector"], clock["tensor"] + LATENCY) + 2.08 * w + 64
            job += 1
            if job in step_end:
                put(("maxima", step_end[job]))
        elif kind == "maxima":
            clock["vector"] += 100
            max_ready[item[1]] = clock["vector"] + SPLIT_MAXIMA
        elif kind == "probs":
            w = BLK - P * max(0, item[4] - TPB * item[2])
            clock["tensor"] += 0.42 * w + 3
            clock["scalar"] = max(clock["scalar"], clock["tensor"] + LATENCY) + 0.83 * w + 52
            ring[turns % 3] = clock["scalar"] + 60
            turns += 1
            exp_done[item[2:5]] = clock["scalar"] + LATENCY + (600 if item[4] >= TPB * item[2] else 0)
        elif kind == "values":
            clock["tensor"] += 1.83 * (BLK - P * max(0, item[4] - TPB * item[2]))
        elif kind in costs:
            tensor, reader, read, after = costs[kind]
            clock["tensor"] += tensor
            clock[reader] = max(clock[reader], clock["tensor"] + LATENCY) + read
            ring[turns % 3] = clock[reader] + 60
            clock[reader] += after
            turns += 1
            if kind in ("q_in", "k_in"):
                clock["scalar"] = max(clock["scalar"], clock["tensor"]) + 571
            if kind == "maxrows":
                max_placed[item[1]] = clock["tensor"] + PLACE_MAXIMA
                max_ready.pop(item[1])
        elif kind == "keep":
            clock["scalar"] += 478
        elif kind == "norm1":
            clock["vector"] += 260

    for b in range(2):
        for kind in PREPARE:
            plan.append((kind, b))
    while main:
        item, due = main[0]
        for s in sorted(max_ready):
            if max_ready[s] <= clock["tensor"]:
                put(("maxrows", s))
        if item[0] == "probs":
            s = G * item[2] + item[3]
            if job < sum(per_step[:s + 1]):
                put(("scores", job, *jobs[job]))
                continue
        if job < len(jobs):
            scores = ("scores", job, *jobs[job])
            stands = start_of(scores) - start_of(item)
            if (job < due and (stands <= PATIENCE or due - job >= HOLD)) or (job < due + EAGER and stands < -PATIENCE):
                put(scores)
                continue
        if item[0] == "probs" and s in max_ready:
            put(("maxrows", s))
        put(main.pop(0)[0])
    put(value)
    put(("keep", G * NB - 1))
    return plan, finish


def block_kernel(nc, x, Wq, bq, Wk, bk, Wv, bv, Wo, bo, router_w, w_gate, w_up, w_down,
                 s_gate, s_up, s_down, out):
    _, T, D = x.shape
    H, HD = 16, 8
    G = H // 4
    NB, NT = T // BLK, T // P
    E, _, FF = w_gate.shape
    FC = FF // P
    NE = E + 1
    WAVES = ((0, NB - 1), (NB - 1, NB))
    tiles = [(TPB * a, TPB * b) for a, b in WAVES]
    sorted_tiles, NX = [], 0
    for a, b in tiles:
        n = ((b - a) * P + E * (P - 1)) // P
        sorted_tiles.append((NX, NX + n))
        NX += n
    wave_of = lambda k: next(w for w, (a, b) in enumerate(sorted_tiles) if a <= k < b)
    wave_blocks = {b: w for w, (lo, hi) in enumerate(WAVES) for b in range(lo, hi)}
    most_tiles = max(b - a for a, b in tiles)
    most_sorted = max(b - a for a, b in sorted_tiles)
    SCALE = float(HD) ** -0.5
    STACK = PARTS * PARTS * HD
    KROWS = 96
    VC = HD + 1
    assert D == P and H * HD == D and STACK + PARTS <= KROWS

    plan, tail = make_plan(NB, G)
    n_units = sum(1 for i in plan if i[0] == "probs")

    def experts(w):
        lo, hi = sorted_tiles[w]
        steps = []
        for k in range(lo - AHEAD - GATHER_AHEAD, hi + 1):
            step = [(kind, k + lag) for kind, lag in (("gather", AHEAD + GATHER_AHEAD), ("sorted_in", AHEAD), ("gate_up", AHEAD - 1),
                                                      ("hid_turn", 0), ("expert_out", -1)) if lo <= k + lag < hi]
            steps.append(step)
        return steps

    first_wave = experts(0)
    pieces = [[("mix_consts",)]] + [[(k, b)] for b in range(NB - 1) for k in ("x_turn", "route")]
    pieces += [[("positions", 0)]] + [[]] * ORDER_AFTER + [[("order", 0)]]
    quads = [i for i, it in enumerate(plan) if it[0] == "values" and it[2] == NB - 1]
    early = [(q + ROUTE_AT, p) for q, p in enumerate(pieces)]
    early += [(EXPERTS_AT + n, first_wave.pop(0)) for n in range(EARLY)]
    early.sort(key=lambda e: e[0])
    for q, piece in reversed(early):
        plan[quads[q] + 1:quads[q] + 1] = piece

    moe = []
    shared = [("shared", n // 2, n % 2) for n in range(2 * NB)]
    for b in range(NB):
        shared.insert(3 * b + 3, ("shared_out", b))
    mine = [it for it in shared if it[0:2] == ("shared", NB - 1)]
    before_mine = shared.index(mine[0])
    filler = first_wave + [[it] for it in shared[:before_mine]]

    def fill(n):
        for _ in range(n):
            if filler:
                moe.extend(filler.pop(0))

    T0 = NT - TPB
    for t in range(T0, NT + 3):
        for kind, lag in (("heads_turn", 0), ("out_turn", 1), ("norm1", 3), ("out_proj", 2)):
            if T0 <= t - lag < NT:
                moe.append((kind, t - lag))
                fill(FILL[0] if kind != "norm1" else 0)
    fill(FILL[4])
    moe += [("return", 0), ("x_turn", NB - 1)]
    fill(FILL[1])
    filler += [[it] for it in shared[before_mine:]]
    moe.append(("route", NB - 1))
    fill(FILL[2])
    moe += [("return", 1), ("positions", 1)]
    fill(FILL[3])
    moe.append(("order", 1))
    fill(len(filler) - 1)
    between = [(SHARED_OUT_AT, filler.pop()[0]), (RETURN_AT, ("return", 2))] + [
        (MOMENTS_AT + (3 * b + n) // 2, (kind, b)) for b in range(NB - 1) for n, kind in enumerate(("add2", "stats2", "aggr2"))]
    for n, step in enumerate(experts(1)):
        moe.extend(step)
        moe += [it for at, it in between if at == n]
    moe += [("rstd2",), ("return", NB - 1)] + [("norm2", b) for b in range(NB - 1)]
    for T0 in range(NT - TPB, NT):
        moe.append(("last_moments", T0))
        if T0 > NT - TPB:
            moe.append(("last_norm", T0 - 1))
    moe.append(("last_norm", NT - 1))
    plan = plan + moe

    ring_kinds = ("probs", "q_in", "k_in", "x_in", "v_in", "maxrows", "heads_turn", "out_turn", "out_proj",
                  "x_turn", "route", "shared_out", "positions", "order", "sorted_in", "hid_turn", "expert_out")
    bank_of, held_before, holder, given = {}, {}, {}, {}
    last_job = max(n for n, it in enumerate(plan) if it[0] == "scores")
    last_values = max(n for n, it in enumerate(plan) if it[0] == "values")
    for n, it in enumerate(plan):
        late = last_job < n <= last_values
        if it[0] == "scores":
            choices = [(it[1] % 2 * 2, it[1] % 2 * 2 + 1)]
        elif it in (("x_in", 0), ("v_in", 0)):
            choices = [(7,)] if it[0] == "x_in" else [(0,)]
        elif it[0] in ring_kinds:
            choices = [(4,), (5,), (6,)] + ([(0,), (1,)] if late else [])
        elif it[0] == "gate_up":
            choices = [(2,), (3,)] + ([] if late else [(0,), (1,)])
        elif it[0] == "shared":
            choices = [(0, 1), (2, 3)]
        else:
            continue
        mine = min(choices, key=lambda c: max(given.get(b, -1) for b in c))
        bank_of[it] = mine[0]
        held_before[it] = sorted({holder[b] for b in mine if b in holder})
        for b in mine:
            holder[b], given[b] = it, n

    def upto(kind, item):
        return [it for it in plan if it[0] == kind].index(item) + 1

    ctx = ExitStack()
    with ctx:
        def sb(name, shape, dt):
            return ctx.enter_context(nc.sbuf_tensor(name, shape, dt))

        def sem(name):
            return ctx.enter_context(nc.semaphore(name))

        ident = sb("ident", [P, P], F32)
        ident_bf = sb("ident_bf", [P, P], BF16)
        mask_qk = sb("mask_qk", [P, P], BF16)
        x_sb = sb("x_sb", [P, NT, D], F32)
        xT = sb("xT", [P, 2, BLK], F32)
        wT = sb("wT", [P, 4, D], F32)
        rT = sb("rT", [P, E], F32)
        bias_qk = sb("bias_qk", [P, 2], F32)
        bias_vo = sb("bias_vo", [P, 2, D], F32)
        qk_f = sb("qk_f", [P, 2, 2, BLK], F32)
        qk_parts = sb("qk_parts", [P, 2, 2, PARTS, BLK], BF16)
        q_stack = sb("q_stack", [P, 2, H, BLK], BF16)
        k_stack = sb("k_stack", [P, NB, H, BLK], BF16)
        v_aug = sb("v_aug", [P, NT, H * VC + 32 - VC], F32)
        probs = sb("probs", [P, RING, BLK], F32)
        part_max = sb("part_max", [P, 2, TPB, 4, NB], F32)
        row_max = sb("row_max", [P, 2, TPB, 4], F32)
        max_parts = sb("max_parts", [P, 2, TPB, PARTS, 4], BF16)
        max_rows = sb("max_rows", [PARTS * 4, 2, BLK], BF16)
        oT = sb("oT", [P, 2, G, BLK], F32)
        w_nat = oT[:, 0, 0, :].rearrange("p (i d) -> p i d", i=4)
        r_nat = oT[0:E, 0, 1, 0:D]
        denom_inv = sb("denom_inv", [P, H], F32)
        o_norm = sb("o_norm", [P, 2, H, HD], F32)
        o_normT = sb("o_normT", [P, 2, P], F32)
        stats = sb("stats", [P, TPB, 6], F32)
        moments1 = sb("moments1", [P, TPB, 2], F32)
        rstd1 = sb("rstd1", [P, TPB], F32)
        minus_half = sb("minus_half", [P, NT - TPB], F32)
        w_gu = sb("w_gu", [P, NE, 2 * FF], F32)
        wd = sb("wd", [P, NE, FC, D], F32)
        x1T = [xT[:, 0, :], xT[:, 1, :], qk_f[:, 0, 0, :], qk_f[:, 0, 1, :]]
        xs = qk_f[:, 1, 0, :].rearrange("p (t d) -> p t d", t=TPB)
        logits = sb("logits", [P, TPB, E], F32)
        top = sb("top", [P, TPB], F32)
        best = sb("best", [P, TPB], F32)
        rank = sb("rank", [P, TPB, E], F32)
        order = sb("order", [P, E], F32)
        score = sb("score", [P, TPB], F32)
        hot = sb("hot", [P, NT, E], BF16)
        hot_before = sb("hot_before", [P, NT + len(WAVES), E], BF16)
        after_q = q_stack[:, (NB - 1) % 2 ^ 1, :, :].rearrange("p h t -> p (h t)").bitcast(F32)
        after_parts = qk_parts[:, :, :, :, :].rearrange("p s b a t -> p (s b a t)").bitcast(F32)
        after_k = k_stack[:, :, :, :].rearrange("p b h t -> p (b h t)").bitcast(F32)

        def carve(region, shapes):
            at, made = 0, []
            for *shape, dt in shapes:
                n = 1
                for d in shape:
                    n *= d
                words = (n + 1) // 2 if dt in (F16, BF16) else n
                words += -words % 8
                view = region[:, at:at + words]
                view = view if dt == F32 else view.bitcast(dt)
                view = view[:, 0:n]
                names = "abc"[:len(shape)]
                sizes = dict(zip(names, shape))
                made.append(view.rearrange(f"p ({' '.join(names)}) -> p {' '.join(names)}", **sizes))
                at += words
            assert at <= region.shape[1]
            return made

        (xg, xgT, x_hid) = carve(after_parts, [(8, D, F32), (4, P, F32), (4, FF, F32)])
        (x_hidT, x_out, column, tile_no, full_tiles, lower, token, counts, n_tiles, start, end, base, expert_f,
         slot_f, place_f, tile_f, expert_i, slot_i, place_i, tile_i, source_i, earlier, ones_bf, filled, summed,
         slots, before, place_hot, tile_hot) = carve(after_q, [
            (2, FF, F32), (4, D, F32), (P, F32), (most_sorted, F32), (most_tiles, F32), (E, E, F32), (NT, F32),
            (E, F32), (E, F32), (E, F32), (E, F32), (E, F32), (most_sorted, F32),
            (most_tiles, F32), (most_tiles, F32), (most_tiles, F32), (NX, I32), (NT, I32), (most_tiles, I32),
            (most_tiles, I32), (NX, I32), (P, BF16), (P, BF16), (E, most_tiles, F32), (E, E, F32),
            (most_tiles, E, F32), (most_sorted, E, F32), (most_tiles, P, F16), (most_tiles, most_sorted, F16)])
        (sig, hid, yg, y_out, moments2, rstd2) = carve(after_k, [
            (2, BLK, F32), (4, BLK, F32), (NT, D, F32), (NT, D, F32), (NT, 2, F32), (NT, F32)])

        parts_dram = nc.dram_tensor("parts_dram", (2, NB, PARTS, P, BLK), BF16, kind="Internal").ap()

        xs_dram = nc.dram_tensor("xs_dram", (T, D), F32, kind="Internal").ap()
        sorted_dram = [nc.dram_tensor(f"sorted_dram{w}", ((b - a) * P, D), F32, kind="Internal").ap()
                       for w, (a, b) in enumerate(sorted_tiles)]

        score_ps = ctx.enter_context(nc.psum_tensor("score_ps", [P, 2, 2, BLK], F32))
        ring_ps = ctx.enter_context(nc.psum_tensor("ring_ps", [P, 3, BLK], F32))
        out_ps = ctx.enter_context(nc.psum_tensor("out_ps", [P, BLK], F32))

        def bank(it, half=0):
            b = bank_of[it] + half
            if b < 4:
                return score_ps[:, b // 2, b % 2, :]
            return ring_ps[:, b - 4, :] if b < 7 else out_ps[:, :]

        x_loaded = [sem(f"x_loaded{b}") for b in range(NB)]
        qk_loaded = sem("qk_loaded")
        vor_loaded = sem("vor_loaded")
        bias_qk_loaded = sem("bias_qk_loaded")
        bias_vo_loaded = sem("bias_vo_loaded")
        first_q_stacked = sem("first_q_stacked")
        first_k_stacked = sem("first_k_stacked")
        moe_loaded = sem("moe_loaded")
        pool_step = sem("pool_step")
        k_filled = sem("k_filled")
        q_filled = sem("q_filled")
        consts_ready = sem("consts_ready")
        w_turned = sem("w_turned")
        w_kept = sem("w_kept")
        x_turned = sem("x_turned")
        x_kept = sem("x_kept")
        qk_made = sem("qk_made")
        first_part_kept = sem("first_part_kept")
        qk_kept = sem("qk_kept")
        v_made = sem("v_made")
        v_kept = sem("v_kept")
        q_split = sem("q_split")
        k_split = sem("k_split")
        bo_added = sem("bo_added")
        q_sent = [sem(f"q_sent{b}") for b in range(NB)]
        k_sent = [sem(f"k_sent{b}") for b in range(NB)]
        q_stacked = [sem(f"q_stacked{b}") for b in range(NB)]
        k_stacked = [sem(f"k_stacked{b}") for b in range(NB)]
        dve_step = sem("dve_step")
        scores_ready = sem("scores_ready")
        scores_read = sem("scores_read")
        maxima_step = sem("maxima_step")
        max_made = sem("max_made")
        max_ready = sem("max_ready")
        max_turned = sem("max_turned")
        max_rows_kept = sem("max_rows_kept")
        max_rows_placed = [sem(f"max_rows_placed{i}") for i in range(2)]
        logits_ready = sem("logits_ready")
        exp_in_ready = sem("exp_in_ready")
        probs_ready = sem("probs_ready")
        probs_masked = sem("probs_masked")
        values_done = sem("values_done")
        out_kept = sem("out_kept")
        heads_turned = sem("heads_turned")
        heads_normed = sem("heads_normed")
        out_turned = sem("out_turned")
        out_turn_kept = sem("out_turn_kept")
        out_projected = sem("out_projected")
        x1_ready = sem("x1_ready")
        y_made = sem("y_made")
        var1_ready = sem("var1_ready")
        rstd1_ready = sem("rstd1_ready")
        var2_ready = sem("var2_ready")
        rstd2_ready = sem("rstd2_ready")
        x1_turned = sem("x1_turned")
        x1T_kept = sem("x1T_kept")
        logits_read = sem("logits_read")
        top_ready = sem("top_ready")
        score_tanh = sem("score_tanh")
        xs_ready = sem("xs_ready")
        xs_stored = [sem(f"xs_stored{b}") for b in range(NB)]
        hot_ready = sem("hot_ready")
        hot_summed = sem("hot_summed")
        mix_consts = sem("mix_consts")
        shared_made = sem("shared_made")
        shared_tanh = sem("shared_tanh")
        shared_ready = sem("shared_ready")
        shared_out_made = sem("shared_out_made")
        shared_added = sem("shared_added")
        positions_made = sem("positions_made")
        positions_read = sem("positions_read")
        places_ready = sem("places_ready")
        experts_ready = sem("experts_ready")
        order_made = sem("order_made")
        order_ready = sem("order_ready")
        gathered = [sem(f"gathered{k}") for k in range(8)]
        sorted_turned = sem("sorted_turned")
        sorted_kept = [sem(f"sorted_kept{w}") for w in range(len(WAVES))]
        gate_up_made = sem("gate_up_made")
        gate_tanh = sem("gate_tanh")
        expert_hid_ready = sem("expert_hid_ready")
        hid_turned = sem("hid_turned")
        hid_kept = sem("hid_kept")
        expert_out_made = sem("expert_out_made")
        expert_out_kept = [sem(f"expert_out_kept{w}") for w in range(len(WAVES))]
        expert_out_stored = [sem(f"expert_out_stored{i}") for i in range(4)]
        returned = [sem(f"returned{t}") for t in range(NT)]
        last_var_ready = sem("last_var_ready")
        last_rstd_ready = sem("last_rstd_ready")
        last_y_ready = sem("last_y_ready")
        y_ready = sem("y_ready")
        y_stored = sem("y_stored")

        def of_wave(signals, k):
            w = wave_of(k)
            return signals[w], k - sorted_tiles[w][0]

        block = ctx.enter_context(nc.Block())

        x_tiles = x.rearrange("a (n p) d -> p (a n) d", p=P)
        out_tiles = out.rearrange("a (n p) d -> p (a n) d", p=P)

        STACKED = 16
        CLEARED = 16

        units_before = {B: sum(1 for it in plan if it[0] == "probs" and it[2] < B) for B in range(NB + 1)}

        def last_quad(s):
            B, g = divmod(s, G)
            return next(it[1:] for it in plan if it[0] == "values" and it[2:] == (B, g, TPB * (B + 1) - 1))

        @block.sync
        def _(sp):
            sp.dma_start(x_sb[:, 0:TPB, :], x_tiles[:, 0:TPB, :]).then_inc(x_loaded[0], 16)
            sp.dma_start(w_nat[:, 1, :], Wk).then_inc(qk_loaded, 16)
            sp.dma_start(bias_qk[:, 1:2], bk.rearrange("(h d) -> d h", d=HD),
                         allow_slow_non_contiguous=True).then_inc(bias_qk_loaded, 16)
            sp.dma_start(w_nat[:, 3, :], Wo).then_inc(vor_loaded, 16)
            sp.dma_start(r_nat, router_w).then_inc(vor_loaded, 16)
            for b in range(1, NB):
                sp.dma_start(x_sb[:, TPB * b:TPB * b + TPB, :],
                             x_tiles[:, TPB * b:TPB * b + TPB, :]).then_inc(x_loaded[b], 16)

            def send(side, b):
                sp.wait_ge((q_split, k_split)[side], b + 1)
                sp.dma_start(parts_dram[side, b].rearrange("a p t -> p a t"),
                             qk_parts[:, side, b % 2, :, :]).then_inc((q_sent, k_sent)[side][b], 16)

            def stack_q(b, heads, stacked):
                sp.wait_ge(q_filled, min(b, 1) + 1)
                if b >= 2:
                    sp.wait_ge(exp_in_ready, units_before[b - 1])
                    sp.dma_start(q_stack[STACK:STACK + PARTS, b % 2, :, :],
                                 q_stack[STACK + PARTS:STACK + 2 * PARTS, b % 2, :, :]).then_inc(stacked, 16)
                sp.wait_ge(q_sent[b], 16)
                rows = parts_dram[0, b].rearrange("a (o d h) t -> o (a d) h t", o=1, d=HD)[:, :, heads, :]
                sp.dma_start(q_stack[0:STACK, b % 2, heads, :].rearrange("p h t -> p (h t)"),
                             rows.rearrange("o p h t -> o p (h t)").to_broadcast(
                                 [PARTS, PARTS * HD, (heads.stop - heads.start) * BLK])).then_inc(stacked, 16)

            def stack_k(b, heads, stacked):
                sp.wait_ge(k_filled, b + 1)
                sp.wait_ge(k_sent[b], 16)
                for r in range(PARTS):
                    rows = parts_dram[1, b, r].rearrange("(o d h) t -> o d h t", o=1, d=HD)[:, :, heads, :]
                    sp.dma_start(k_stack[r * PARTS * HD:(r + 1) * PARTS * HD, b, heads, :].rearrange("p h t -> p (h t)"),
                                 rows.rearrange("o d h t -> o d (h t)").to_broadcast(
                                     [PARTS, HD, (heads.stop - heads.start) * BLK])).then_inc(stacked, 16)

            def load_experts():
                for half, (w, s) in enumerate(((w_gate, s_gate), (w_up, s_up))):
                    columns = slice(half * FF, (half + 1) * FF)
                    sp.dma_start(w_gu[:, 0:E, columns], w.rearrange("e d f -> d e f")).then_inc(moe_loaded, 16)
                    sp.dma_start(w_gu[:, E, columns], s).then_inc(moe_loaded, 16)
                for e in range(E):
                    sp.dma_start(wd[:, e, :, :], w_down[e].rearrange("(c p) d -> p c d", p=P)).then_inc(moe_loaded, 16)
                sp.dma_start(wd[:, E, :, :], s_down.rearrange("(c p) d -> p c d", p=P)).then_inc(moe_loaded, 16)

            send(0, 0)
            send(1, 0)
            stack_q(0, slice(0, 4), first_q_stacked)
            stack_k(0, slice(0, 4), first_k_stacked)
            stack_q(0, slice(4, H), q_stacked[0])
            stack_k(0, slice(4, H), k_stacked[0])
            send(0, 1)
            send(1, 1)
            for it in plan:
                if it[0] == "v_in" and it[1] >= 2:
                    send(0, it[1])
                    send(1, it[1])
                    stack_q(it[1], slice(0, H), q_stacked[it[1]])
                    stack_k(it[1], slice(0, H), k_stacked[it[1]])
                elif it[0] == "maxrows":
                    s = it[1]
                    B, g = divmod(s, G)
                    sp.wait_ge(max_rows_kept, s + 1)
                    sp.dma_start(q_stack[STACK:STACK + PARTS, B % 2, 4 * g:4 * g + 4, :],
                                 max_rows[:, s % 2, :]).then_inc(max_rows_placed[s % 2], 16)
                    if s == 0:
                        stack_q(1, slice(0, H), q_stacked[1])
                        stack_k(1, slice(0, H), k_stacked[1])
                        load_experts()
                elif it[0] == "route":
                    b = it[1]
                    sp.wait_ge(xs_ready, b + 1)
                    sp.dma_start(xs_dram[b * BLK:(b + 1) * BLK, :].rearrange("(t p) d -> p t d", p=P),
                                 xs[:, :, :]).then_inc(xs_stored[b], 16)
                elif it[0] == "expert_out":
                    k = it[1]
                    kept, n = of_wave(expert_out_kept, k)
                    sp.wait_ge(kept, n + 1)
                    row = (k - sorted_tiles[wave_of(k)][0]) * P
                    sp.dma_start(sorted_dram[wave_of(k)][row:row + P, :], x_out[:, k % 4, :]).then_inc(expert_out_stored[k % 4], 16)
                elif it[0] == "norm2":
                    b = it[1]
                    sp.wait_ge(y_ready, b + 1)
                    sp.dma_start(out_tiles[:, TPB * b:TPB * b + TPB, :],
                                 y_out[:, TPB * b:TPB * b + TPB, :]).then_inc(y_stored, 16)
                elif it[0] == "last_norm":
                    T0 = it[1]
                    sp.wait_ge(last_y_ready, T0 - (NT - TPB) + 1)
                    sp.dma_start(out_tiles[:, T0, :], y_out[:, T0, :]).then_inc(y_stored, 16)
            sp.wait_ge(y_stored, 16 * (NB - 1 + TPB))

        @block.gpsimd
        def _(pool):
            chain = [0]

            def link(ins):
                chain[0] += 1
                ins.then_inc(maxima_step, 1)
                pool.wait_ge(maxima_step, chain[0])

            pool.memset(ident[:, :], 0.0).then_inc(pool_step, 1)
            pool.memset(mask_qk[:, :], 0.0).then_inc(pool_step, 1)
            pool.wait_ge(pool_step, 2)
            pool.affine_select(out=ident[:, :], in_=ident[:, :], compare_op=ALU.not_equal, fill=1.0,
                               base=0, pattern=[[-1, P]], channel_multiplier=1).then_inc(pool_step, 1)
            pool.wait_ge(pool_step, 3)
            pool.tensor_copy(ident_bf[:, :], ident[:, :]).then_inc(pool_step, 1)
            pool.affine_select(out=mask_qk[:, :], in_=mask_qk[:, :], compare_op=ALU.is_ge, fill=MASKED,
                               base=0, pattern=[[-1, P]], channel_multiplier=1).then_inc(pool_step, 1)
            for i, bias in enumerate((bv, bo)):
                pool.dma_start(bias_vo[:, i, :], bias.rearrange("(a d) -> a d", a=1).to_broadcast([P, D])
                               ).then_inc(bias_vo_loaded, 16)
            pool.wait_ge(pool_step, 5)
            for b in range(NB):
                minus_ones = k_stack[64:96, b, :, :].bitcast(F32)
                pool.memset(minus_ones, MINUS_ONES).then_inc(k_filled, 1)
                pool.wait_ge(k_filled, b + 1)
                if b == 0:
                    pool.memset(v_aug[:, :, :], 1.0).then_inc(consts_ready, 1)
                    pool.wait_ge(consts_ready, 1)
                    pool.memset(q_stack[64:96, 1, :, :].bitcast(F32), 0.0).then_inc(q_filled, 1)
                    pool.wait_ge(q_filled, 2)
            for e in range(E):
                pool.memset(order[:, e:e + 1], float(E - e)).then_inc(consts_ready, 1)
            for w, (a, b) in enumerate(tiles):
                pool.memset(hot_before[:, a + w, :], 0.0).then_inc(consts_ready, 1)
            steps = 5
            pool.memset(minus_half[:, :], -0.5).then_inc(pool_step, 1)
            steps += 1
            pool.wait_ge(pool_step, steps)
            pool.wait_ge(bias_vo_loaded, 32)
            for it in plan:
                kind = it[0]
                if kind == "v_in":
                    b = it[1]
                    pool.wait_ge(x_turned, b + 1)
                    here = x_sb[:, TPB * b:TPB * b + TPB, :]
                    pool.tensor_tensor(here, here, bias_vo[:, 1:2, :].to_broadcast([P, TPB, D]),
                                       ALU.add).then_inc(bo_added, 1)
                elif kind == "probs":
                    _, n, B, g, j, i = it
                    if i == 3 and j >= TPB * B:
                        pool.wait_ge(probs_ready, n + 1)
                        first = (n - 3) % RING
                        square = probs[:, first:first + 4, 0:P]
                        pool.affine_select(out=square, in_=square, compare_op=ALU.is_ge, fill=0.0, base=0,
                                           pattern=[[0, 4], [1, P]], channel_multiplier=-1).then_inc(probs_masked, 1)
                elif kind == "maxima":
                    s = it[1]
                    pool.wait_ge(max_made, s + 1)
                    if s >= 2:
                        pool.wait_ge(max_turned, s - 1)
                    rest = row_max[:, s % 2, :, :]
                    for a in range(PARTS):
                        part = max_parts[:, s % 2, :, a, :]
                        copied = pool.tensor_copy(part, rest)
                        if a == PARTS - 1:
                            copied.then_inc(max_ready, 1)
                            break
                        link(copied)
                        link(pool.tensor_tensor(rest, rest, part, ALU.subtract))
                elif kind == "out_proj":
                    T0 = it[1]
                    pool.wait_ge(var1_ready, T0 + 1)
                    pool.tensor_tensor(rstd1[:, T0 % TPB:T0 % TPB + 1], rstd1[:, T0 % TPB:T0 % TPB + 1],
                                       minus_half[:, 0:1], ALU.pow).then_inc(rstd1_ready, 1)
                elif kind == "mix_consts":
                    pool.wait_ge(exp_in_ready, units_before[NB - 1])
                    pool.wait_ge(q_sent[NB - 1], 16)
                    pool.wait_ge(k_sent[NB - 1], 16)
                    pool.iota(column[:, :], [[1, P]], base=0, channel_multiplier=0,
                              allow_small_or_imprecise_dtypes=True).then_inc(mix_consts, 1)
                    pool.iota(tile_no[:, :], [[1, most_sorted]], base=0, channel_multiplier=0,
                              allow_small_or_imprecise_dtypes=True).then_inc(mix_consts, 1)
                    pool.iota(full_tiles[:, :], [[P, most_tiles]], base=0, channel_multiplier=0,
                              allow_small_or_imprecise_dtypes=True).then_inc(mix_consts, 1)
                    pool.iota(token[:, :], [[P, NT]], base=0, channel_multiplier=1,
                              allow_small_or_imprecise_dtypes=True).then_inc(mix_consts, 1)
                    pool.memset(lower[:, :, :], 1.0).then_inc(mix_consts, 1)
                    pool.memset(ones_bf[:, :], 1.0).then_inc(mix_consts, 1)
                    pool.wait_ge(mix_consts, 6)
                    pool.affine_select(out=earlier[:, :], in_=ones_bf[:, :], compare_op=ALU.is_ge, fill=0.0, base=-1,
                                       pattern=[[1, P]], channel_multiplier=-1).then_inc(mix_consts, 1)
                    pool.affine_select(out=lower[:, :, :], in_=lower[:, :, :], compare_op=ALU.is_ge, fill=0.0,
                                       base=-1, pattern=[[1, E], [-1, E]], channel_multiplier=0).then_inc(mix_consts, 1)
                elif kind == "route":
                    b = it[1]
                    pool.wait_ge(hot_ready, b + 1)
                    if b == 0:
                        pool.wait_ge(consts_ready, 1 + E + len(WAVES))
                    w = wave_blocks[b]
                    for t in range(TPB * b, TPB * b + TPB):
                        pool.tensor_tensor(hot_before[:, t + w + 1, :], hot_before[:, t + w, :], hot[:, t, :],
                                           ALU.add).then_inc(hot_summed, 1)
                        pool.wait_ge(hot_summed, t + 1)
                elif kind == "gather":
                    k = it[1]
                    w = wave_of(k)
                    if k == sorted_tiles[w][0]:
                        pool.wait_ge(order_ready, w + 1)
                        for b in range(*WAVES[w]):
                            pool.wait_ge(xs_stored[b], 16)
                    if k >= 8:
                        pool.wait_ge(sorted_turned, k - 7)
                        pool.wait_ge(gathered[k % 8], 16 * (k // 8))
                    pool.indirect_dma_start(
                        out=xg[:, k % 8, :], out_offset=None, in_=xs_dram[0:P * tiles[w][1], :],
                        in_offset=bass.IndirectOffsetOnAxis(ap=source_i[:, k:k + 1], axis=0),
                        bounds_check=P * tiles[w][1] - 1).then_inc(gathered[k % 8], 16)
                elif kind == "return":
                    b = it[1]
                    w = wave_blocks[b]
                    if b == WAVES[w][0]:
                        pool.wait_ge(exp_in_ready, n_units)
                        for i in range(4):
                            pool.wait_ge(expert_out_stored[i], 16 * len(range(i, sorted_tiles[w][1], 4)))
                    for t in range(TPB * b, TPB * b + TPB):
                        pool.indirect_dma_start(
                            out=yg[:, t, :], out_offset=None, in_=sorted_dram[w][:, :],
                            in_offset=bass.IndirectOffsetOnAxis(ap=slot_i[:, t:t + 1], axis=0),
                            bounds_check=sorted_dram[w].shape[0] - 1).then_inc(returned[t], 16)
                elif kind == "rstd2":
                    n = NT - TPB
                    pool.wait_ge(var2_ready, NB - 1)
                    pool.tensor_tensor(rstd2[:, 0:n], rstd2[:, 0:n], minus_half[:, 0:n], ALU.pow).then_inc(rstd2_ready, 1)
                elif kind == "last_moments":
                    T0 = it[1]
                    pool.wait_ge(last_var_ready, T0 - (NT - TPB) + 1)
                    pool.tensor_tensor(rstd2[:, T0:T0 + 1], rstd2[:, T0:T0 + 1], minus_half[:, 0:1],
                                       ALU.pow).then_inc(last_rstd_ready, 1)

        @block.scalar
        def _(act):
            act.dma_start(w_nat[:, 0, :], Wq).then_inc(qk_loaded, 16)
            act.dma_start(bias_qk[:, 0:1], bq.rearrange("(h d) -> d h", d=HD),
                          allow_slow_non_contiguous=True).then_inc(bias_qk_loaded, 16)
            act.dma_start(w_nat[:, 2, :], Wv).then_inc(vor_loaded, 16)
            act.wait_ge(w_turned, 1)
            for i in range(2):
                act.activation(wT[:, i, :].rearrange("p (d h) -> p d h", d=HD),
                               score_ps[:, 1, 0, i * D:(i + 1) * D].rearrange("p (h d) -> p d h", d=HD), ACT.Copy).then_inc(w_kept, 1)
            for it in plan:
                kind = it[0]
                if kind == "x_in":
                    b = it[1]
                    act.wait_ge(x_turned, b + 1)
                    act.activation(xT[:, b % 2, :], bank(it), ACT.Copy).then_inc(x_kept, 1)
                elif kind in ("q_in", "k_in"):
                    b = it[1]
                    side = int(kind == "k_in")
                    act.wait_ge(qk_made, 2 * b + side + 1)
                    if b == 0:
                        act.wait_ge(bias_qk_loaded, 32)
                    if b >= 2:
                        act.wait_ge((q_sent, k_sent)[side][b - 2], 16)
                    act.activation(qk_parts[:, side, b % 2, 0, :], bank(it), ACT.Identity,
                                   bias=bias_qk[:, side:side + 1]).then_inc(first_part_kept, 1)
                    if it == ("k_in", 0):
                        act.wait_ge(w_turned, 2)
                        act.activation(wT[:, 2:4, :], score_ps[:, 1, 0, 2 * D:4 * D].rearrange("p (i d) -> p i d", i=2),
                                       ACT.Copy).then_inc(w_kept, 1)
                        act.activation(rT[:, :], score_ps[:, 1, 1, 0:E], ACT.Copy).then_inc(w_kept, 1)
                elif kind == "probs":
                    _, n, B, g, j, i = it
                    w = BLK - P * max(0, j - TPB * B)
                    act.wait_ge(exp_in_ready, n + 1)
                    if n >= RING:
                        act.wait_ge(values_done, (n - RING) // 4 + 1)
                    act.activation(probs[:, n % RING, 0:w], bank(it)[:, 0:w], ACT.Exp,
                                   scale=SCALE).then_inc(probs_ready, 1)
                elif kind == "maxrows":
                    s = it[1]
                    act.wait_ge(max_turned, s + 1)
                    if s >= 2:
                        act.wait_ge(max_rows_placed[s % 2], 16 * (s // 2))
                    act.activation(max_rows[:, s % 2, :], bank(it)[0:4 * PARTS, :], ACT.Copy).then_inc(max_rows_kept, 1)
                elif kind == "keep":
                    s = it[1]
                    B, g = divmod(s, G)
                    act.wait_ge(values_done, upto("values", ("values", *last_quad(s))))
                    if B >= 2:
                        act.wait_ge(heads_turned, TPB * (B - 1))
                    act.activation(oT[:, B % 2, g, :], out_ps[:, :], ACT.Copy).then_inc(out_kept, 1)
                elif kind == "out_turn":
                    act.wait_ge(out_turned, it[1] + 1)
                    if it[1] >= 2:
                        act.wait_ge(out_projected, it[1] - 1)
                    act.activation(o_normT[:, it[1] % 2, :], bank(it)[:, 0:P], ACT.Copy).then_inc(out_turn_kept, 1)
                elif kind == "x_turn":
                    b = it[1]
                    act.wait_ge(x1_turned, b + 1)
                    act.activation(x1T[b], bank(it), ACT.Copy).then_inc(x1T_kept, 1)
                elif kind == "route":
                    b = it[1]
                    act.wait_ge(top_ready, b + 1)
                    act.activation(score[:, :], top[:, :], ACT.Tanh, scale=0.5).then_inc(score_tanh, 1)
                elif kind == "shared":
                    _, b, f = it
                    r = b * FC + f
                    act.wait_ge(shared_made, r + 1)
                    if r >= 2:
                        act.wait_ge(shared_ready, r - 1)
                    act.activation(sig[:, r % 2, :], bank(it), ACT.Tanh,
                                   scale=0.5).then_inc(shared_tanh, 1)
                elif kind == "sorted_in" and wave_of(it[1]) == 1:
                    k = it[1]
                    act.wait_ge(sorted_turned, k + 1)
                    act.wait_ge(gate_up_made, k - 3)
                    act.activation(xgT[:, k % 4, :], bank(it)[:, 0:P], ACT.Copy).then_inc(sorted_kept[1], 1)
                elif kind == "expert_out" and wave_of(it[1]) == 1:
                    k = it[1]
                    act.wait_ge(expert_out_made, k + 1)
                    act.wait_ge(expert_out_stored[k % 4], 16 * (k // 4))
                    act.activation(x_out[:, k % 4, :], bank(it)[:, 0:D], ACT.Copy, scale=0.5).then_inc(expert_out_kept[1], 1)
                elif kind == "gate_up":
                    k = it[1]
                    act.wait_ge(gate_up_made, k + 1)
                    if k >= 4:
                        act.wait_ge(hid_turned, k - 3)
                    act.activation(x_hid[:, k % 4, :], bank(it)[:, 0:FF], ACT.Tanh,
                                   scale=0.5).then_inc(gate_tanh, 1)
                elif kind == "hid_turn":
                    k = it[1]
                    act.wait_ge(hid_turned, k + 1)
                    if k >= 2:
                        act.wait_ge(expert_out_made, k - 1)
                    act.activation(x_hidT[:, k % 2, :], bank(it)[:, 0:FF], ACT.Copy).then_inc(hid_kept, 1)

        @block.vector
        def _(dve):
            chain = [0]

            def link(ins):
                chain[0] += 1
                ins.then_inc(dve_step, 1)
                dve.wait_ge(dve_step, chain[0])

            def stats_of(first, n):
                for t in range(first, first + n):
                    last = dve.bn_stats(stats[:, t % TPB, :], x_sb[:, t, :])
                return last

            def moments_of(mean_var, var_eps, first, n):
                for t in range(n):
                    last = dve.bn_aggr(mean_var[:, t, :], stats[:, (first + t) % TPB, :])
                link(last)
                return dve.tensor_scalar(var_eps, mean_var[:, :, 1], LN_EPS, None, ALU.add)

            def normalised(mean_var, rstd, dst, src):
                return dve.tensor_scalar(dst, src, mean_var[:, 0:1], rstd, ALU.subtract, ALU.mult)

            dve.memset(q_stack[64:96, 0, :, :].bitcast(F32), 0.0).then_inc(q_filled, 1)
            for it in plan:
                kind = it[0]
                if kind in ("q_in", "k_in"):
                    b = it[1]
                    side = int(kind == "k_in")
                    dve.wait_ge(first_part_kept, 2 * b + side + 1)
                    rest = qk_f[:, side, b % 2, :]
                    parts = qk_parts[:, side, b % 2, :, :]
                    dve.scalar_tensor_tensor(out=rest, in0=bank(it), scalar=bias_qk[:, side:side + 1], in1=parts[:, 0, :],
                                             op0=ALU.add, op1=ALU.subtract).then_inc(qk_kept, 1)
                    dve.wait_ge(qk_kept, 2 * b + side + 1)
                    link(dve.tensor_copy(parts[:, 1, :], rest))
                    link(dve.tensor_tensor(rest, rest, parts[:, 1, :], ALU.subtract))
                    dve.tensor_copy(parts[:, 2, :], rest).then_inc((q_split, k_split)[side], 1)
                elif kind == "v_in":
                    b = it[1]
                    dve.wait_ge(v_made, b + 1)
                    if b == 0:
                        dve.wait_ge(bias_vo_loaded, 32)
                    dve.wait_ge(consts_ready, 1)
                    for t in range(TPB):
                        dst = v_aug[:, TPB * b + t, 0:H * VC].rearrange("p (h c) -> p h c", c=VC)[:, :, 0:HD]
                        last = dve.tensor_tensor(
                            dst, bank(it)[:, t * P:(t + 1) * P].rearrange("p (h c) -> p h c", c=HD),
                            bias_vo[:, 0, :].rearrange("p (h c) -> p h c", c=HD), ALU.add)
                    last.then_inc(v_kept, 1)
                elif kind == "scores":
                    _, m, B, g, t, c, hp = it
                    w = min(BLK, P * (TPB * B + t + 1) - BLK * c)
                    s = G * B + g
                    dve.wait_ge(scores_ready, m + 1)
                    dve.tensor_reduce(out=part_max[:, s % 2, t, 2 * hp:2 * hp + 2, c], in_=score_ps[:, m % 2, :, 0:w],
                                      axis=AX.X, op=ALU.max).then_inc(scores_read, 1)
                elif kind == "maxima":
                    s = it[1]
                    B = s // G
                    dve.wait_ge(scores_read, sum(2 * TPB * (q // G + 1) for q in range(s + 1)))
                    if s >= 2:
                        dve.wait_ge(max_ready, s - 1)
                    dve.tensor_reduce(out=row_max[:, s % 2, :, :], in_=part_max[:, s % 2, :, :, 0:B + 1],
                                      axis=AX.X, op=ALU.max).then_inc(max_made, 1)
                elif kind == "heads_turn":
                    T0 = it[1]
                    dve.wait_ge(heads_turned, T0 + 1)
                    by_head = bank(it).rearrange("p (h c) -> p h c", c=32)
                    link(dve.reciprocal(denom_inv[:, :], by_head[:, :, HD]))
                    if T0 >= 2:
                        dve.wait_ge(out_turned, T0 - 1)
                    dve.tensor_tensor(o_norm[:, T0 % 2, :, :], by_head[:, :, 0:HD],
                                      denom_inv[:, :].rearrange("p (h c) -> p h c", c=1).to_broadcast([P, H, HD]),
                                      ALU.mult).then_inc(heads_normed, 1)
                elif kind == "out_proj":
                    T0 = it[1]
                    dve.wait_ge(out_projected, T0 + 1)
                    dve.wait_ge(bo_added, T0 // TPB + 1)
                    dve.tensor_tensor(x_sb[:, T0, :], bank(it)[:, 0:D], x_sb[:, T0, :], ALU.add).then_inc(y_made, 1)
                    dve.wait_ge(y_made, T0 + 1)
                    i = T0 % TPB
                    link(stats_of(T0, 1))
                    moments_of(moments1[:, i:i + 1, :], rstd1[:, i:i + 1], T0, 1).then_inc(var1_ready, 1)
                elif kind == "norm1":
                    T0 = it[1]
                    dve.wait_ge(rstd1_ready, T0 + 1)
                    i = T0 % TPB
                    normalised(moments1[:, i, :], rstd1[:, i:i + 1], x_sb[:, T0, :], x_sb[:, T0, :]).then_inc(x1_ready, 1)
                elif kind == "route":
                    b = it[1]
                    dve.wait_ge(x1_ready, TPB * (b + 1))
                    dve.wait_ge(logits_ready, b + 1)
                    dve.tensor_copy(logits[:, :, :], bank(it)[:, 0:TPB * E].rearrange("p (t e) -> p t e", e=E)).then_inc(logits_read, 1)
                    dve.wait_ge(logits_read, b + 1)
                    if b >= 1:
                        dve.wait_ge(xs_ready, b)
                    dve.tensor_reduce(out=top[:, :], in_=logits[:, :, :], axis=AX.X, op=ALU.max).then_inc(top_ready, 1)
                    dve.wait_ge(top_ready, b + 1)
                    spread = lambda v: v.rearrange("p (t a) -> p t a", a=1).to_broadcast([P, TPB, E])
                    link(dve.tensor_tensor(rank[:, :, :], logits[:, :, :], spread(top[:, :]), ALU.is_equal))
                    if b == 0:
                        dve.wait_ge(consts_ready, 1 + E)
                    link(dve.tensor_tensor(rank[:, :, :], rank[:, :, :],
                                           order[:, :].rearrange("p (a e) -> p a e", a=1).to_broadcast([P, TPB, E]), ALU.mult))
                    link(dve.tensor_reduce(out=best[:, :], in_=rank[:, :, :], axis=AX.X, op=ALU.max))
                    dve.tensor_tensor(hot[:, TPB * b:TPB * b + TPB, :], rank[:, :, :], spread(best[:, :]),
                                      ALU.is_equal).then_inc(hot_ready, 1)
                    dve.wait_ge(score_tanh, b + 1)
                    if b >= 1:
                        dve.wait_ge(xs_stored[b - 1], 16)
                    link(dve.tensor_scalar(score[:, :], score[:, :], 0.5, 0.5, ALU.mult, ALU.add))
                    for t in range(TPB):
                        last = dve.tensor_scalar(xs[:, t, :], x_sb[:, TPB * b + t, :], score[:, t:t + 1], None, ALU.mult)
                    last.then_inc(xs_ready, 1)
                elif kind == "shared":
                    _, b, f = it
                    r = b * FC + f
                    dve.wait_ge(shared_tanh, r + 1)
                    link(dve.scalar_tensor_tensor(out=sig[:, r % 2, :], in0=sig[:, r % 2, :], scalar=1.0,
                                                  in1=bank(it), op0=ALU.add, op1=ALU.mult))
                    if r >= 4:
                        dve.wait_ge(shared_out_made, r // FC - 1)
                    dve.tensor_tensor(hid[:, r % 4, :], sig[:, r % 2, :], bank(it, 1),
                                      ALU.mult).then_inc(shared_ready, 1)
                elif kind == "shared_out":
                    b = it[1]
                    dve.wait_ge(shared_out_made, b + 1)
                    so_far = x_sb[:, TPB * b:TPB * b + TPB, :].rearrange("p t d -> p (t d)")
                    dve.scalar_tensor_tensor(out=so_far, in0=bank(it), scalar=0.5, in1=so_far,
                                             op0=ALU.mult, op1=ALU.add).then_inc(shared_added, 1)
                elif kind == "positions":
                    w = it[1]
                    (lo, hi), (x_lo, x_hi) = tiles[w], sorted_tiles[w]
                    n, nx = hi - lo, x_hi - x_lo
                    dve.wait_ge(positions_made, w + 1)
                    dve.wait_ge(mix_consts, 8)

                    def over(v, n, inner):
                        m = v.shape[1]
                        if inner:
                            return v.rearrange("p (m a) -> p m a", a=1).to_broadcast([P, m, n])
                        return v.rearrange("p (a m) -> p a m", a=1).to_broadcast([P, n, m])

                    pos = bank(it)[:, 0:n * E].rearrange("p (t e) -> p t e", e=E)
                    link(dve.tensor_copy(counts, bank(it)[:, n * E:n * E + E]))
                    link(dve.tensor_tensor(filled[:, :, 0:n], over(counts, n, True), over(full_tiles[:, 0:n], E, False), ALU.is_gt))
                    link(dve.tensor_reduce(out=n_tiles, in_=filled[:, :, 0:n], axis=AX.X, op=ALU.add))
                    link(dve.tensor_tensor(summed, lower, over(n_tiles, E, False), ALU.mult))
                    link(dve.tensor_reduce(out=start, in_=summed, axis=AX.X, op=ALU.add))
                    dve.tensor_tensor(end, start, n_tiles, ALU.add)
                    link(dve.tensor_scalar(base, start, float(P), None, ALU.mult))
                    dve.tensor_tensor(slots[:, 0:n, :], pos, over(base, n, False), ALU.add).then_inc(positions_read, 1)
                    dve.wait_ge(positions_read, w + 1)
                    dve.tensor_tensor(before[:, 0:nx, :], over(tile_no[:, 0:nx], E, True), over(end, nx, False), ALU.is_ge)
                    link(dve.tensor_tensor(slots[:, 0:n, :], slots[:, 0:n, :], hot[:, lo:hi, :], ALU.mult))
                    dve.tensor_reduce(out=expert_f[:, 0:nx], in_=before[:, 0:nx, :], axis=AX.X, op=ALU.add)
                    link(dve.tensor_reduce(out=slot_f[:, 0:n], in_=slots[:, 0:n, :], axis=AX.X, op=ALU.add))
                    dve.tensor_scalar(expert_i[:, x_lo:x_hi], expert_f[:, 0:nx], float(E - 1), None, ALU.min).then_inc(experts_ready, 1)
                    link(dve.tensor_copy(slot_i[:, lo:hi], slot_f[:, 0:n]))
                    dve.tensor_scalar(place_i[:, 0:n], slot_i[:, lo:hi], P - 1, None, ALU.bitwise_and)
                    link(dve.tensor_scalar(tile_i[:, 0:n], slot_i[:, lo:hi], P.bit_length() - 1, None, ALU.logical_shift_right))
                    dve.tensor_copy(place_f[:, 0:n], place_i[:, 0:n])
                    link(dve.tensor_copy(tile_f[:, 0:n], tile_i[:, 0:n]))
                    link(dve.tensor_tensor(tile_hot[:, 0:n, 0:nx], over(tile_f[:, 0:n], nx, True), over(tile_no[:, 0:nx], n, False),
                                           ALU.is_equal))
                    dve.tensor_tensor(tile_hot[:, 0:n, 0:nx], tile_hot[:, 0:n, 0:nx], over(token[:, lo:hi], nx, True), ALU.mult)
                    dve.tensor_tensor(place_hot[:, 0:n, :], over(place_f[:, 0:n], P, True), over(column, n, False),
                                      ALU.is_equal).then_inc(places_ready, 1)
                elif kind == "order":
                    w = it[1]
                    x_lo, x_hi = sorted_tiles[w]
                    dve.wait_ge(order_made, w + 1)
                    dve.tensor_copy(source_i[:, x_lo:x_hi], bank(it)[:, 0:x_hi - x_lo]).then_inc(order_ready, 1)
                elif kind == "sorted_in" and wave_of(it[1]) == 0:
                    k = it[1]
                    dve.wait_ge(sorted_turned, k + 1)
                    if k >= 4:
                        dve.wait_ge(gate_up_made, k - 3)
                    dve.tensor_copy(xgT[:, k % 4, :], bank(it)[:, 0:P]).then_inc(sorted_kept[0], 1)
                elif kind == "expert_out" and wave_of(it[1]) == 0:
                    k = it[1]
                    dve.wait_ge(expert_out_made, k + 1)
                    if k >= 4:
                        dve.wait_ge(expert_out_stored[k % 4], 16 * (k // 4))
                    dve.tensor_scalar(x_out[:, k % 4, :], bank(it)[:, 0:D], 0.5, None, ALU.mult).then_inc(expert_out_kept[0], 1)
                elif kind == "gate_up":
                    k = it[1]
                    dve.wait_ge(gate_tanh, k + 1)
                    both = bank(it)
                    link(dve.scalar_tensor_tensor(out=x_hid[:, k % 4, :], in0=x_hid[:, k % 4, :], scalar=1.0,
                                                  in1=both[:, 0:FF], op0=ALU.add, op1=ALU.mult))
                    dve.tensor_tensor(x_hid[:, k % 4, :], x_hid[:, k % 4, :], both[:, FF:2 * FF],
                                      ALU.mult).then_inc(expert_hid_ready, 1)
                elif kind == "add2":
                    b = it[1]
                    mine = slice(TPB * b, TPB * (b + 1))
                    for t in range(TPB * b, TPB * (b + 1)):
                        dve.wait_ge(returned[t], 16)
                    dve.wait_ge(shared_added, b + 1)
                    link(dve.tensor_tensor(x_sb[:, mine, :], x_sb[:, mine, :], yg[:, mine, :], ALU.add))
                elif kind == "stats2":
                    link(stats_of(TPB * it[1], TPB))
                elif kind == "aggr2":
                    mine = slice(TPB * it[1], TPB * (it[1] + 1))
                    moments_of(moments2[:, mine, :], rstd2[:, mine], TPB * it[1], TPB).then_inc(var2_ready, 1)
                elif kind == "norm2":
                    b = it[1]
                    dve.wait_ge(rstd2_ready, 1)
                    for t in range(TPB * b, TPB * b + TPB):
                        last = normalised(moments2[:, t, :], rstd2[:, t:t + 1], y_out[:, t, :], x_sb[:, t, :])
                    last.then_inc(y_ready, 1)
                elif kind == "last_moments":
                    T0 = it[1]
                    dve.wait_ge(returned[T0], 16)
                    dve.wait_ge(shared_added, NB)
                    link(dve.tensor_tensor(x_sb[:, T0, :], x_sb[:, T0, :], yg[:, T0, :], ALU.add))
                    link(stats_of(T0, 1))
                    moments_of(moments2[:, T0:T0 + 1, :], rstd2[:, T0:T0 + 1], T0, 1).then_inc(last_var_ready, 1)
                elif kind == "last_norm":
                    T0 = it[1]
                    dve.wait_ge(last_rstd_ready, T0 - (NT - TPB) + 1)
                    normalised(moments2[:, T0, :], rstd2[:, T0:T0 + 1], y_out[:, T0, :], x_sb[:, T0, :]).then_inc(last_y_ready, 1)

        @block.tensor
        def _(pe):
            mm, turn = pe.matmul, pe.transpose

            pe.wait_ge(pool_step, 5)
            pe.wait_ge(qk_loaded, 32)
            for i in range(2):
                last = turn(score_ps[:, 1, 0, i * P:(i + 1) * P], w_nat[:, i, :], ident[:, :])
            last.then_inc(w_turned, 1)

            def wait_bank(it):
                for last in held_before[it]:
                    read = {"probs": probs_ready, "x_in": x_kept, "q_in": qk_kept, "k_in": qk_kept, "v_in": v_kept,
                            "maxrows": max_rows_kept, "heads_turn": heads_normed, "out_turn": out_turn_kept,
                            "out_proj": y_made, "x_turn": x1T_kept, "route": logits_read,
                            "shared_out": shared_added, "positions": positions_read, "order": order_ready,
                            "sorted_in": sorted_kept, "hid_turn": hid_kept, "expert_out": expert_out_kept,
                            "scores": scores_read, "gate_up": expert_hid_ready, "shared": shared_ready}[last[0]]
                    count = {"shared": FC * last[1] + last[-1], "q_in": 2 * last[1], "k_in": 2 * last[1] + 1}.get(last[0], last[1])
                    if last[0] in ("sorted_in", "expert_out"):
                        read, count = of_wave(read, count)
                    pe.wait_ge(read, count + 1)

            expert = {}

            def load_expert(k):
                expert[k] = pe.value_load(expert_i[0:1, k:k + 1], min_val=0, max_val=E - 1)

            for it in plan:
                kind = it[0]
                if kind == "x_in":
                    b = it[1]
                    if b >= 1:
                        wait_bank(it)
                    pe.wait_ge(x_loaded[b], 16)
                    for t in range(TPB):
                        last = turn(bank(it)[:, t * P:(t + 1) * P], x_sb[:, TPB * b + t, :], ident[:, :])
                    last.then_inc(x_turned, 1)
                elif kind in ("q_in", "k_in"):
                    b = it[1]
                    side = int(kind == "k_in")
                    wait_bank(it)
                    if b == 0:
                        pe.wait_ge(w_kept, side + 1)
                    pe.wait_ge(x_kept, b + 1)
                    mm(bank(it), wT[:, side, :], xT[:, b % 2, :], start=True, stop=True).then_inc(qk_made, 1)
                    if it == ("k_in", 0):
                        pe.wait_ge(vor_loaded, 48)
                        for i in range(2, 4):
                            turn(score_ps[:, 1, 0, i * P:(i + 1) * P], w_nat[:, i, :], ident[:, :])
                        turn(score_ps[:, 1, 1, 0:E], r_nat, ident[0:E, 0:E]).then_inc(w_turned, 1)
                elif kind == "v_in":
                    b = it[1]
                    if b >= 1:
                        wait_bank(it)
                    if b == 0:
                        pe.wait_ge(w_kept, 3)
                    for t in range(TPB):
                        last = mm(bank(it)[:, t * P:(t + 1) * P], xT[:, b % 2, t * P:(t + 1) * P], wT[:, 2, :],
                                  start=True, stop=True)
                    last.then_inc(v_made, 1)
                elif kind == "scores":
                    _, m, B, g, t, c, hp = it
                    T0 = TPB * B + t
                    w = min(BLK, P * (T0 + 1) - BLK * c)
                    if m >= 2:
                        pe.wait_ge(scores_read, m - 1)
                    elif m == 0:
                        pe.wait_ge(v_kept, 1)
                    elif m == 1:
                        pe.wait_ge(w_kept, 4)
                    if B == 0 and g == 0 and t == 0:
                        pe.wait_ge(first_k_stacked, STACKED * PARTS)
                        pe.wait_ge(first_q_stacked, STACKED)
                    elif g == (1 if B == 0 else 0) and t == 0:
                        pe.wait_ge(k_stacked[c], STACKED * PARTS)
                        pe.wait_ge(q_stacked[B], STACKED + (CLEARED if B >= 2 else 0))
                    for i in range(2):
                        h = 4 * g + 2 * hp + i
                        last = mm(score_ps[:, m % 2, i, 0:w], q_stack[0:KROWS, B % 2, h, t * P:(t + 1) * P],
                                  k_stack[0:KROWS, c, h, 0:w], start=True, stop=c < B)
                        if c == B:
                            last = mm(score_ps[:, m % 2, i, w - P:w], ident_bf[:, :], mask_qk[:, :],
                                      start=False, stop=True)
                    last.then_inc(scores_ready, 1)
                elif kind == "maxrows":
                    s = it[1]
                    wait_bank(it)
                    pe.wait_ge(max_ready, s + 1)
                    for t in range(TPB):
                        last = mm(bank(it)[0:4 * PARTS, t * P:(t + 1) * P],
                                  max_parts[:, s % 2, t, :, :].rearrange("p a h -> p (a h)"), ident_bf[:, :],
                                  start=True, stop=True)
                    last.then_inc(max_turned, 1)
                elif kind == "probs":
                    _, n, B, g, j, i = it
                    s = G * B + g
                    skip = P * max(0, j - TPB * B)
                    w = BLK - skip
                    h = 4 * g + i
                    wait_bank(it)
                    if j == 0 and i == 0:
                        pe.wait_ge(max_rows_placed[s % 2], 16 * (s // 2 + 1))
                    mm(bank(it)[:, 0:w], k_stack[0:KROWS, j // TPB, h, j % TPB * P:(j % TPB + 1) * P],
                       q_stack[0:KROWS, B % 2, h, skip:BLK], start=True, stop=True).then_inc(exp_in_ready, 1)
                elif kind == "values":
                    _, k, B, g, j = it
                    s = G * B + g
                    skip = P * max(0, j - TPB * B)
                    w = BLK - skip
                    if j >= TPB * B:
                        pe.wait_ge(probs_masked, TPB * s + j - TPB * B + 1)
                    else:
                        pe.wait_ge(probs_ready, 4 * k + 4)
                    if k == 0:
                        pe.wait_ge(x_kept, 1)
                    if j == 0 and s >= 1:
                        pe.wait_ge(out_kept, s)
                    for i in range(4):
                        h = 4 * g + i
                        last = mm(out_ps[32 * i:32 * i + 32, skip:BLK], v_aug[:, j, h * VC:h * VC + 32],
                                  probs[:, (4 * k + i) % RING, 0:w], start=j == 0, stop=j == TPB * (B + 1) - 1)
                    last.then_inc(values_done, 1)
                elif kind == "heads_turn":
                    T0 = it[1]
                    B, t = divmod(T0, TPB)
                    wait_bank(it)
                    pe.wait_ge(out_kept, G * (B + 1))
                    for g in range(G):
                        last = turn(bank(it)[:, g * P:(g + 1) * P], oT[:, B % 2, g, t * P:(t + 1) * P], ident[:, :])
                    last.then_inc(heads_turned, 1)
                elif kind == "out_turn":
                    wait_bank(it)
                    pe.wait_ge(heads_normed, it[1] + 1)
                    turn(bank(it)[:, 0:P], o_norm[:, it[1] % 2, :, :].rearrange("p h c -> p (h c)"), ident[:, :]).then_inc(out_turned, 1)
                elif kind == "out_proj":
                    wait_bank(it)
                    pe.wait_ge(out_turn_kept, it[1] + 1)
                    mm(bank(it)[:, 0:D], o_normT[:, it[1] % 2, :], wT[:, 3, :], start=True, stop=True).then_inc(out_projected, 1)
                elif kind == "x_turn":
                    b = it[1]
                    wait_bank(it)
                    pe.wait_ge(x1_ready, TPB * (b + 1))
                    for t in range(TPB):
                        last = turn(bank(it)[:, t * P:(t + 1) * P], x_sb[:, TPB * b + t, :], ident[:, :])
                    last.then_inc(x1_turned, 1)
                elif kind == "route":
                    b = it[1]
                    wait_bank(it)
                    pe.wait_ge(x1T_kept, b + 1)
                    for t in range(TPB):
                        last = mm(bank(it)[:, t * E:(t + 1) * E], x1T[b][:, t * P:(t + 1) * P], rT[:, :],
                                  start=True, stop=True)
                    last.then_inc(logits_ready, 1)
                elif kind == "shared":
                    _, b, f = it
                    r = b * FC + f
                    wait_bank(it)
                    pe.wait_ge(x1T_kept, b + 1)
                    for half in range(2):
                        at = half * FF + f * P
                        last = mm(bank(it, half), w_gu[:, E, at:at + P], x1T[b], start=True, stop=True)
                    last.then_inc(shared_made, 1)
                elif kind == "shared_out":
                    b = it[1]
                    wait_bank(it)
                    pe.wait_ge(shared_ready, FC * (b + 1))
                    for t in range(TPB):
                        for f in range(FC):
                            last = mm(bank(it)[:, t * P:(t + 1) * P], hid[:, (FC * b + f) % 4, t * P:(t + 1) * P],
                                      wd[:, E, f, :], start=f == 0, stop=f == FC - 1)
                    last.then_inc(shared_out_made, 1)
                elif kind == "positions":
                    w = it[1]
                    lo, hi = tiles[w]
                    n = hi - lo
                    wait_bank(it)
                    pe.wait_ge(hot_summed, hi)
                    pe.wait_ge(mix_consts, 8)
                    mm(bank(it)[:, 0:n * E], earlier[:, :], hot[:, lo:hi, :].rearrange("p t e -> p (t e)"), start=True, stop=False)
                    mm(bank(it)[:, 0:n * E], ones_bf[:, :], hot_before[:, lo + w:hi + w, :].rearrange("p t e -> p (t e)"),
                       start=False, stop=True)
                    mm(bank(it)[:, n * E:n * E + E], ones_bf[:, :], hot_before[:, hi + w, :],
                       start=True, stop=True).then_inc(positions_made, 1)
                elif kind == "order":
                    w = it[1]
                    n, nx = tiles[w][1] - tiles[w][0], sorted_tiles[w][1] - sorted_tiles[w][0]
                    wait_bank(it)
                    pe.wait_ge(places_ready, w + 1)
                    for t in range(n):
                        last = mm(bank(it)[:, 0:nx], place_hot[:, t, :], tile_hot[:, t, 0:nx], start=t == 0, stop=t == n - 1)
                    last.then_inc(order_made, 1)
                    pe.wait_ge(experts_ready, w + 1)
                    load_expert(sorted_tiles[w][0])
                elif kind == "sorted_in":
                    k = it[1]
                    wait_bank(it)
                    pe.wait_ge(gathered[k % 8], 16 * (k // 8 + 1))
                    turn(bank(it)[:, 0:P], xg[:, k % 8, :], ident[:, :]).then_inc(sorted_turned, 1)
                elif kind == "gate_up":
                    k = it[1]
                    wait_bank(it)
                    if k == 0:
                        pe.wait_ge(moe_loaded, 16 * (4 + NE))
                    kept, n = of_wave(sorted_kept, k)
                    pe.wait_ge(kept, n + 1)
                    e = expert[k]
                    mm(bank(it), xgT[:, k % 4, :], w_gu[:, bass.ds(e, 1), :].rearrange("p a n -> p (a n)"),
                       start=True, stop=True).then_inc(gate_up_made, 1)
                    if k + 1 < sorted_tiles[wave_of(k)][1]:
                        load_expert(k + 1)
                elif kind == "hid_turn":
                    k = it[1]
                    wait_bank(it)
                    pe.wait_ge(expert_hid_ready, k + 1)
                    for f in range(FC):
                        last = turn(bank(it)[:, f * P:(f + 1) * P], x_hid[:, k % 4, f * P:(f + 1) * P], ident[:, :])
                    last.then_inc(hid_turned, 1)
                elif kind == "expert_out":
                    k = it[1]
                    wait_bank(it)
                    pe.wait_ge(hid_kept, k + 1)
                    e = expert[k]
                    for f in range(FC):
                        last = mm(bank(it)[:, 0:D], x_hidT[:, k % 2, f * P:(f + 1) * P],
                                  wd[:, bass.ds(e, 1), f, :].rearrange("p a n -> p (a n)"), start=f == 0, stop=f == FC - 1)
                    last.then_inc(expert_out_made, 1)


_INS = ['L0_attn_x', 'L0_attn_Wq', 'L0_attn_bq', 'L0_attn_Wk', 'L0_attn_bk', 'L0_attn_Wv', 'L0_attn_bv',
        'L0_attn_Wo', 'L0_attn_bo', 'L0_ffn_router_w', 'L0_ffn_expert_gate', 'L0_ffn_expert_up',
        'L0_ffn_expert_down', 'L0_ffn_shared_gate', 'L0_ffn_shared_up', 'L0_ffn_shared_down']
_OUTS = [((1, 2048, 128), 'float32')]


def kernel(**inputs):
    import numpy as _np
    import concourse.bacc as _bacc
    from concourse import mybir as _mybir
    from concourse.bass_utils import run_bass_kernel_spmd as _run

    nc = _bacc.Bacc("TRN2", target_bir_lowering=False, num_devices=1)
    arrays, args = {}, []
    for name in _INS:
        a = _np.ascontiguousarray(inputs[name])
        arrays[f"in_{name}_dram"] = a
        args.append(nc.dram_tensor(f"in_{name}_dram", a.shape, _mybir.dt.from_np(a.dtype), kind="ExternalInput").ap())
    for i, (shape, dtype) in enumerate(_OUTS):
        dt = _mybir.dt.from_np(_np.dtype(dtype))
        args.append(nc.dram_tensor(f"out_{i}_dram", shape, dt, kind="ExternalOutput").ap())
    block_kernel(nc, *args)
    r = _run(nc, [arrays], core_ids=[0])
    got = tuple(r.results[0][f"out_{i}_dram"] for i in range(len(_OUTS)))
    return got[0]
```
